# Optimizing a Trainium2 kernel written in Bass

```python
import numpy as np
import jax
import jax.numpy as jnp

def _softmax(x, axis=-1):
    return jax.nn.softmax(x, axis=axis)

def _gelu(x):
    return jax.nn.gelu(x, approximate=True)

def _silu(x):
    return jax.nn.silu(x)

def _sigmoid(x):
    return jax.nn.sigmoid(x)

def _layernorm(x, axis=-1, eps=1e-05):
    m = jnp.mean(x, axis=axis, keepdims=True)
    v = jnp.var(x, axis=axis, keepdims=True)
    return (x - m) / jnp.sqrt(v + eps)

def _scatter_add(tgt, idx, src, axis=0):
    return tgt.at[idx].add(src)

def _segment_sum(src, seg, n):
    return jax.ops.segment_sum(src, seg, n)
kernel_name = 'mk_flamingo_gated_d2_seqx_r8_975eb1'

def setup_inputs(seed: int=0):
    np.random.seed(seed)
    _w = jnp.asarray

    def _rec_inputs():
        import jax
        import jax.numpy as jnp
        _rk = jax.random.key(seed)
        x = -0.0002928 + 1 * jax.random.normal(jax.random.fold_in(_rk, 1), (8, 128, 128), jnp.float32)
        _lenS = 128 - jax.random.randint(jax.random.fold_in(_rk, 7), (8,), 0, max(1, 128 // 4) + 1, jnp.int32)
        _lenS2 = 128 - jax.random.randint(jax.random.fold_in(_rk, 8), (8,), 0, max(1, 128 // 4) + 1, jnp.int32)
        _ctx_1024P = jax.random.normal(jax.random.fold_in(_rk, 11), (8, 16, 128), jnp.float32)
        _ctx_1024c = jax.random.dirichlet(jax.random.fold_in(_rk, 511), 0.3 * jnp.ones((16,), jnp.float32), (8, 128))
        _ctx_1024t = jnp.einsum('bsk,bkd->bsd', _ctx_1024c, _ctx_1024P)
        _ctx_1024t = _ctx_1024t * jax.lax.rsqrt(jnp.mean(jnp.square(_ctx_1024t)) + 1e-12) * 0.953939
        ctx_1024 = -1.39393e-06 + 0.999914 * (_ctx_1024t + 0.3 * jax.random.normal(jax.random.fold_in(_rk, 611), (8, 128, 128), jnp.float32))
        _g = jax.random.normal(jax.random.fold_in(_rk, 9001), (2, 2), jnp.float32)
        _g = jnp.sign(_g) * jnp.maximum(jnp.abs(_g), 1.0) + (_g == 0) * 1.0
        g_xattn = _g[0]
        g_ffn = _g[1]
        return (x, ctx_1024, g_xattn, g_ffn)
    x, ctx_1024, g_xattn, g_ffn = _rec_inputs()

    def _L0_xattn_setup():
        import jax, jax.numpy as jnp
        import numpy as np
        D_MODEL = 128
        N_HEADS = 16
        D_K = D_MODEL // N_HEADS
        LOCAL_WINDOW = 128
        GLOBAL_TOKENS = 16

        def sparse_mask(seq_len):
            i = jnp.arange(seq_len)[:, None]
            j = jnp.arange(seq_len)[None, :]
            local = jnp.abs(i - j) <= LOCAL_WINDOW
            glob = (i < GLOBAL_TOKENS) | (j < GLOBAL_TOKENS)
            causal = j <= i
            return ((local | glob) & causal)[None, None]
        key = jax.random.key(seed)
        ks = jax.random.split(key, 11)
        B, S = (2, 256)
        std = 1.0 / np.sqrt(D_MODEL)
        inp = {'query': jax.random.normal(ks[0], (B, S, D_MODEL), jnp.float32), 'key': jax.random.normal(ks[1], (B, S, D_MODEL), jnp.float32), 'value': jax.random.normal(ks[2], (B, S, D_MODEL), jnp.float32), 'w_q': jax.random.normal(ks[3], (D_MODEL, D_MODEL), jnp.float32) * std, 'b_q': jnp.zeros((D_MODEL,), jnp.float32), 'w_k': jax.random.normal(ks[4], (D_MODEL, D_MODEL), jnp.float32) * std, 'b_k': jnp.zeros((D_MODEL,), jnp.float32), 'w_v': jax.random.normal(ks[5], (D_MODEL, D_MODEL), jnp.float32) * std, 'b_v': jnp.zeros((D_MODEL,), jnp.float32), 'w_o': jax.random.normal(ks[6], (D_MODEL, D_MODEL), jnp.float32) * std, 'b_o': jnp.zeros((D_MODEL,), jnp.float32)}
        return inp
    _L0_xattn_all = _L0_xattn_setup()
    _L0_xattn_in = {k: v for k, v in _L0_xattn_all.items() if k in ('w_q', 'b_q', 'w_k', 'b_k', 'w_v', 'b_v', 'w_o', 'b_o')}
    del _L0_xattn_all

    def _L0_ffn_setup():
        import jax, jax.numpy as jnp
        import numpy as np
        HIDDEN = 128
        INNER = 512

        def _weight_quant(w):
            scale = 1.0 / jnp.clip(jnp.mean(jnp.abs(w)), 1e-05)
            wq = jnp.clip(jnp.round(w * scale), -1.0, 1.0) / scale
            return w + jax.lax.stop_gradient(wq - w)

        def _act_quant(x):
            scale = 127.0 / jnp.clip(jnp.max(jnp.abs(x), axis=-1, keepdims=True), 1e-05)
            xq = jnp.clip(jnp.round(x * scale), -128.0, 127.0) / scale
            return x + jax.lax.stop_gradient(xq - x)

        def _bitlinear(x, w):
            return jnp.einsum('bsi,oi->bso', _act_quant(x), _weight_quant(w))
        key = jax.random.key(seed)
        k0, k1, k2, k3 = jax.random.split(key, 4)
        x = jax.random.normal(k0, (4, 256, HIDDEN), dtype=jnp.float32)
        w_gate = jax.random.normal(k1, (INNER, HIDDEN), dtype=jnp.float32) / np.sqrt(HIDDEN)
        w_up = jax.random.normal(k2, (INNER, HIDDEN), dtype=jnp.float32) / np.sqrt(HIDDEN)
        w_down = jax.random.normal(k3, (HIDDEN, INNER), dtype=jnp.float32) / np.sqrt(INNER)
        return {'x': x, 'w_gate': w_gate, 'w_up': w_up, 'w_down': w_down}
    _L0_ffn_all = _L0_ffn_setup()
    _L0_ffn_in = {k: v for k, v in _L0_ffn_all.items() if k in ('w_gate', 'w_up', 'w_down')}
    del _L0_ffn_all

    def _L1_xattn_setup():
        import jax, jax.numpy as jnp
        import numpy as np
        E = 128
        H = 16
        D = E // H
        key = jax.random.key(seed)
        ks = jax.random.split(key, 12)
        B, Tq, Tk = (2, 128, 1024)
        s = 0.02
        return {'hidden_states': jax.random.normal(ks[0], (B, Tq, E), jnp.float32), 'key_value_states': jax.random.normal(ks[1], (B, Tk, E), jnp.float32), 'Wq': jax.random.normal(ks[2], (E, E), jnp.float32) * s, 'bq': jnp.zeros((E,), jnp.float32), 'Wk': jax.random.normal(ks[3], (E, E), jnp.float32) * s, 'bk': jnp.zeros((E,), jnp.float32), 'Wv': jax.random.normal(ks[4], (E, E), jnp.float32) * s, 'bv': jnp.zeros((E,), jnp.float32), 'Wo': jax.random.normal(ks[5], (E, E), jnp.float32) * s, 'bo': jnp.zeros((E,), jnp.float32), 'stride': 16}
    _L1_xattn_all = _L1_xattn_setup()
    _L1_xattn_in = {k: v for k, v in _L1_xattn_all.items() if k in ('Wq', 'bq', 'Wk', 'bk', 'Wv', 'bv', 'Wo', 'bo')}
    del _L1_xattn_all

    def _L1_ffn_setup():
        import jax, jax.numpy as jnp
        import numpy as np
        DIM = 128
        MOE_HID = 64
        SHARED_HID = 256
        N_EXPERTS = 16
        TOP_K = 2
        NORM_TOPK_PROB = True
        key = jax.random.key(seed)
        ks = jax.random.split(key, 9)
        s = 0.02
        x = jax.random.normal(ks[0], (2, 128, DIM), dtype=jnp.float32)
        Wg = jax.random.normal(ks[1], (N_EXPERTS, DIM), dtype=jnp.float32) * s
        We_gate = jax.random.normal(ks[2], (N_EXPERTS, MOE_HID, DIM), dtype=jnp.float32) * s
        We_up = jax.random.normal(ks[3], (N_EXPERTS, MOE_HID, DIM), dtype=jnp.float32) * s
        We_down = jax.random.normal(ks[4], (N_EXPERTS, DIM, MOE_HID), dtype=jnp.float32) * s
        Ws_gate = jax.random.normal(ks[5], (SHARED_HID, DIM), dtype=jnp.float32) * s
        Ws_up = jax.random.normal(ks[6], (SHARED_HID, DIM), dtype=jnp.float32) * s
        Ws_down = jax.random.normal(ks[7], (DIM, SHARED_HID), dtype=jnp.float32) * s
        Wsg = jax.random.normal(ks[8], (1, DIM), dtype=jnp.float32) * s
        return {'x': x, 'Wg': Wg, 'We_gate': We_gate, 'We_up': We_up, 'We_down': We_down, 'Ws_gate': Ws_gate, 'Ws_up': Ws_up, 'Ws_down': Ws_down, 'Wsg': Wsg}
    _L1_ffn_all = _L1_ffn_setup()
    _L1_ffn_in = {k: v for k, v in _L1_ffn_all.items() if k in ('Wg', 'We_gate', 'We_up', 'We_down', 'Ws_gate', 'Ws_up', 'Ws_down', 'Wsg')}
    del _L1_ffn_all
    return {'x': x, 'ctx_1024': ctx_1024, 'g_xattn': g_xattn, 'g_ffn': g_ffn, 'L0_xattn_w_q': _L0_xattn_in['w_q'], 'L0_xattn_b_q': _L0_xattn_in['b_q'], 'L0_xattn_w_k': _L0_xattn_in['w_k'], 'L0_xattn_b_k': _L0_xattn_in['b_k'], 'L0_xattn_w_v': _L0_xattn_in['w_v'], 'L0_xattn_b_v': _L0_xattn_in['b_v'], 'L0_xattn_w_o': _L0_xattn_in['w_o'], 'L0_xattn_b_o': _L0_xattn_in['b_o'], 'L0_ffn_w_gate': _L0_ffn_in['w_gate'], 'L0_ffn_w_up': _L0_ffn_in['w_up'], 'L0_ffn_w_down': _L0_ffn_in['w_down'], 'L1_xattn_Wq': _L1_xattn_in['Wq'], 'L1_xattn_bq': _L1_xattn_in['bq'], 'L1_xattn_Wk': _L1_xattn_in['Wk'], 'L1_xattn_bk': _L1_xattn_in['bk'], 'L1_xattn_Wv': _L1_xattn_in['Wv'], 'L1_xattn_bv': _L1_xattn_in['bv'], 'L1_xattn_Wo': _L1_xattn_in['Wo'], 'L1_xattn_bo': _L1_xattn_in['bo'], 'L1_ffn_Wg': _L1_ffn_in['Wg'], 'L1_ffn_We_gate': _L1_ffn_in['We_gate'], 'L1_ffn_We_up': _L1_ffn_in['We_up'], 'L1_ffn_We_down': _L1_ffn_in['We_down'], 'L1_ffn_Ws_gate': _L1_ffn_in['Ws_gate'], 'L1_ffn_Ws_up': _L1_ffn_in['Ws_up'], 'L1_ffn_Ws_down': _L1_ffn_in['Ws_down'], 'L1_ffn_Wsg': _L1_ffn_in['Wsg']}

def reference(x, ctx_1024, g_xattn, g_ffn, L0_xattn_w_q, L0_xattn_b_q, L0_xattn_w_k, L0_xattn_b_k, L0_xattn_w_v, L0_xattn_b_v, L0_xattn_w_o, L0_xattn_b_o, L0_ffn_w_gate, L0_ffn_w_up, L0_ffn_w_down, L1_xattn_Wq, L1_xattn_bq, L1_xattn_Wk, L1_xattn_bk, L1_xattn_Wv, L1_xattn_bv, L1_xattn_Wo, L1_xattn_bo, L1_ffn_Wg, L1_ffn_We_gate, L1_ffn_We_up, L1_ffn_We_down, L1_ffn_Ws_gate, L1_ffn_Ws_up, L1_ffn_Ws_down, L1_ffn_Wsg):
    import jax
    import jax.numpy as jnp

    def _L0_xattn_ref(query, key, value, w_q, b_q, w_k, b_k, w_v, b_v, w_o, b_o):
        import jax, jax.numpy as jnp
        import numpy as np
        D_MODEL = 128
        N_HEADS = 16
        D_K = D_MODEL // N_HEADS
        LOCAL_WINDOW = 128
        GLOBAL_TOKENS = 16

        def sparse_mask(seq_len):
            i = jnp.arange(seq_len)[:, None]
            j = jnp.arange(seq_len)[None, :]
            local = jnp.abs(i - j) <= LOCAL_WINDOW
            glob = (i < GLOBAL_TOKENS) | (j < GLOBAL_TOKENS)
            causal = j <= i
            return ((local | glob) & causal)[None, None]
        B, S, _ = query.shape

        def proj(x, w, b):
            y = x @ w.T + b
            return y.reshape(B, S, N_HEADS, D_K).transpose(0, 2, 1, 3)
        q = proj(query, w_q, b_q)
        k = proj(key, w_k, b_k)
        v = proj(value, w_v, b_v)
        scores = jnp.einsum('bhqd,bhkd->bhqk', q, k) / np.sqrt(D_K).astype(np.float32)
        mask = sparse_mask(S)
        scores = jnp.where(mask, scores, -jnp.inf)
        attn = jax.nn.softmax(scores, axis=-1)
        out = jnp.einsum('bhqk,bhkd->bhqd', attn, v)
        out = out.transpose(0, 2, 1, 3).reshape(B, S, D_MODEL)
        return out @ w_o.T + b_o

    def _L0_ffn_ref(x, w_gate, w_up, w_down):
        import jax, jax.numpy as jnp
        import numpy as np
        HIDDEN = 128
        INNER = 512

        def _weight_quant(w):
            scale = 1.0 / jnp.clip(jnp.mean(jnp.abs(w)), 1e-05)
            wq = jnp.clip(jnp.round(w * scale), -1.0, 1.0) / scale
            return w + jax.lax.stop_gradient(wq - w)

        def _act_quant(x):
            scale = 127.0 / jnp.clip(jnp.max(jnp.abs(x), axis=-1, keepdims=True), 1e-05)
            xq = jnp.clip(jnp.round(x * scale), -128.0, 127.0) / scale
            return x + jax.lax.stop_gradient(xq - x)

        def _bitlinear(x, w):
            return jnp.einsum('bsi,oi->bso', _act_quant(x), _weight_quant(w))
        gate = jax.nn.silu(_bitlinear(x, w_gate))
        up = _bitlinear(x, w_up)
        return _bitlinear(gate * up, w_down)

    def _L1_xattn_ref(hidden_states, key_value_states, Wq, bq, Wk, bk, Wv, bv, Wo, bo, stride):
        import jax, jax.numpy as jnp
        import numpy as np
        E = 128
        H = 16
        D = E // H
        B, Tq, _ = hidden_states.shape
        Tk = key_value_states.shape[1]
        scaling = D ** (-0.5)
        Q = (hidden_states @ Wq.T + bq).reshape(B, Tq, H, D).transpose(0, 2, 1, 3)
        K = (key_value_states @ Wk.T + bk).reshape(B, Tk, H, D).transpose(0, 2, 1, 3)
        V = (key_value_states @ Wv.T + bv).reshape(B, Tk, H, D).transpose(0, 2, 1, 3)
        m = Tk // stride
        idx = jnp.arange(H)[:, None] + stride * jnp.arange(m)[None, :]
        gather = idx[None, :, :, None]
        Kg = jnp.take_along_axis(K, gather, axis=2)
        Vg = jnp.take_along_axis(V, gather, axis=2)
        scores = jnp.einsum('bhqd,bhkd->bhqk', Q, Kg) * scaling
        attn = jax.nn.softmax(scores, axis=-1)
        out = jnp.einsum('bhqk,bhkd->bhqd', attn, Vg)
        out = out.transpose(0, 2, 1, 3).reshape(B, Tq, E)
        return out @ Wo.T + bo

    def _L1_ffn_ref(x, Wg, We_gate, We_up, We_down, Ws_gate, Ws_up, Ws_down, Wsg):
        import jax, jax.numpy as jnp
        import numpy as np
        DIM = 128
        MOE_HID = 64
        SHARED_HID = 256
        N_EXPERTS = 16
        TOP_K = 2
        NORM_TOPK_PROB = True
        B, S, D = x.shape
        xt = x.reshape(-1, D)
        gates = jax.nn.softmax(xt @ Wg.T, axis=-1)
        scores, inds = jax.lax.top_k(gates, TOP_K)
        if NORM_TOPK_PROB:
            scores = scores / jnp.sum(scores, axis=-1, keepdims=True)
        g = jnp.einsum('td,ehd->teh', xt, We_gate)
        u = jnp.einsum('td,ehd->teh', xt, We_up)
        h = jax.nn.silu(g) * u
        y_all = jnp.einsum('teh,edh->ted', h, We_down)
        y_sel = jnp.take_along_axis(y_all, inds[:, :, None], axis=1)
        y = jnp.sum(y_sel * scores[:, :, None], axis=1)
        shared = jax.nn.silu(xt @ Ws_gate.T) * (xt @ Ws_up.T) @ Ws_down.T
        y = y + jax.nn.sigmoid(xt @ Wsg.T) * shared
        return y.reshape(B, S, D)
    x = x + jnp.tanh(g_xattn[0]) * _L0_xattn_ref(_layernorm(x, axis=-1), ctx_1024, ctx_1024, L0_xattn_w_q, L0_xattn_b_q, L0_xattn_w_k, L0_xattn_b_k, L0_xattn_w_v, L0_xattn_b_v, L0_xattn_w_o, L0_xattn_b_o)
    x = x + jnp.tanh(g_ffn[0]) * _L0_ffn_ref(_layernorm(x, axis=-1), L0_ffn_w_gate, L0_ffn_w_up, L0_ffn_w_down)
    x = x + jnp.tanh(g_xattn[1]) * _L1_xattn_ref(_layernorm(x, axis=-1), ctx_1024, L1_xattn_Wq, L1_xattn_bq, L1_xattn_Wk, L1_xattn_bk, L1_xattn_Wv, L1_xattn_bv, L1_xattn_Wo, L1_xattn_bo, 16)
    x = x + jnp.tanh(g_ffn[1]) * _L1_ffn_ref(_layernorm(x, axis=-1), L1_ffn_Wg, L1_ffn_We_gate, L1_ffn_We_up, L1_ffn_We_down, L1_ffn_Ws_gate, L1_ffn_Ws_up, L1_ffn_Ws_down, L1_ffn_Wsg)
    return x

_drawn_inputs = setup_inputs


def setup_inputs(seed=0):
    import zlib

    import numpy as np

    out = dict(_drawn_inputs(seed))
    spreads = {'g_ffn': (-1.0, 0.6),
     'L0_xattn_b_q': (0.0, 0.431),
     'L0_xattn_b_k': (0.0, 0.8),
     'L0_xattn_b_v': (0.0, 0.1),
     'L0_xattn_b_o': (0.0, 0.1),
     'L1_xattn_bq': (0.0, 0.8),
     'L1_xattn_bk': (0.0, 0.8),
     'L1_xattn_bv': (0.0, 0.42),
     'L1_xattn_bo': (0.0, 0.1)}
    factors = {'L1_xattn_Wq': 8.0,
     'L1_xattn_Wk': 8.0,
     'L1_ffn_Wg': 8.0,
     'L1_ffn_We_gate': 8.0,
     'L1_ffn_We_up': 8.0,
     'L1_ffn_We_down': 8.0,
     'L1_ffn_Ws_gate': 8.0,
     'L1_ffn_Ws_up': 8.0,
     'L1_ffn_Ws_down': 8.0,
     'L1_ffn_Wsg': 8.0}
    for name, (base, spread) in spreads.items():
        noise = np.random.default_rng([zlib.crc32(name.encode()), seed]).standard_normal(out[name].shape)
        drawn = base * np.exp(spread * noise) if base else spread * noise
        out[name] = jnp.asarray(drawn.astype(out[name].dtype))
    for name, factor in factors.items():
        out[name] = (out[name] * factor).astype(out[name].dtype)
    return out
```

```python
from contextlib import ExitStack

import numpy as np

import concourse.bass as bass
from concourse import mybir

F32 = mybir.dt.float32
BF16 = mybir.dt.bfloat16
ALU = mybir.AluOpType
ACT = mybir.ActivationFunctionType
AX = mybir.AxisListType

B, S, D = 8, 128, 128
H, DK = 16, 8
NG, NQ = 4, 4
QW = 32
VW = DK + 1
INNER = 512
KEYS = 8
HALF = 4
NE, HID, SHARED = 16, 64, 256
NR = NE + 1
NC = (NE * HID + SHARED) // 128
SCALE = float(DK) ** -0.5
EPS = 1e-5
QMIN = 1e-5
MAGIC = 1.5 * 2.0 ** 23
MASKED = -1e30

A_WQ, A_WK, A_WV, A_WO, A_ID = 0, 512, 1024, 1152, 1280
A_BQ, A_BK, A_BV, A_GX, A_GF = 1408, 1412, 1416, 1417, 1419
A_COLS = 1421
L_WQ, L_WK, L_WV, L_WO, L_MK, L_MV = (128 * k for k in range(6))
L_BQ, L_BK, L_BV = 768, 769, 770
L_COLS = 771


def build(nc, x, ctxT, aw, rows, fw, lw, sel, ew, out):
    es = ExitStack()
    with es:
        def sb(name, shape, dt=F32):
            return es.enter_context(nc.sbuf_tensor(name, shape, dt))

        def sem(name):
            return es.enter_context(nc.semaphore(name))

        bank = [es.enter_context(nc.psum_tensor(f"bank{i}", [128, 512], F32)) for i in range(8)]

        x_all = sb("x_all", [128, B * D])
        cT = sb("cT", [128, B * S])
        a = sb("a", [128, A_COLS])
        bo = sb("bo", [1, 2 * D])
        ones_row = sb("ones_row", [1, S])
        ones_sq = sb("ones_sq", [128, 128])
        maskb = sb("maskb", [128, 128], BF16)
        identb = sb("identb", [128, 128], BF16)
        fws = sb("fws", [128, 3 * INNER])
        lws = sb("lws", [128, L_COLS])
        sels = sb("sels", [3 * NR, NC * 128], BF16)
        ews = sb("ews", [128, NC * 3 * 128 + NR])
        tg = sb("tg", [128, 4])
        stats = sb("stats", [128, B * 6])
        mv = sb("mv", [128, B * 2])
        ve = sb("ve", [128, B])
        mhalf = sb("mhalf", [128, B])
        rstd = sb("rstd", [128, B])
        ident = a[:, A_ID:A_ID + 128]

        vaug = sb("vaug", [128, B * H * VW])
        xn = sb("xn", [128, 2, D])
        xnT = sb("xnT", [128, 2, S])
        kT = sb("kT", [128, 2, NG * S])
        qT = sb("qT", [128, 2, NG * S])
        mx = sb("mx", [128, 2, NQ, NG])
        sx = sb("sx", [128, NQ, NG * S])
        pr = sb("pr", [128, NQ, NG * S])
        pT = sb("pT", [128, 2, NG * S])
        rl = sb("rl", [128, H])
        on = sb("on", [128, D])
        oT = sb("oT", [128, S])

        fabs = sb("fabs", [128, 3])
        fmean = sb("fmean", [128, 3])
        fclip = sb("fclip", [128, 3])
        fscale = sb("fscale", [128, 3])
        fdeq = sb("fdeq", [128, 3])
        fq32 = sb("fq32", [128, 3 * INNER])
        fqc = sb("fqc", [128, 3 * INNER])
        fq = sb("fq", [128, 3, INNER], BF16)
        f_xn = sb("f_xn", [128, D])
        f_t = sb("f_t", [128, D])
        f_xq = sb("f_xq", [128, 2, D], BF16)
        f_a = sb("f_a", [128, 4])
        f_deq = sb("f_deq", [128, 2, 2])
        f_xqT = sb("f_xqT", [128, 2, S], BF16)
        f_sil = sb("f_sil", [128, 2, INNER])
        f_h = sb("f_h", [128, 2, INNER])
        f_ah = sb("f_ah", [128, 2, 5])
        f_ht = sb("f_ht", [128, INNER])
        f_hq = sb("f_hq", [128, 2, INNER], BF16)
        f_hqT = sb("f_hqT", [128, 2, INNER], BF16)

        W = HALF * 128
        kb = sb("kb", [128, 2, W])
        vb = sb("vb", [128, 2, W])
        n3 = sb("n3", [128, 2, W])
        nT3 = sb("nT3", [128, 2, W])
        q3 = sb("q3", [128, 2, W])
        m3 = sb("m3", [128, 2, HALF * H])
        s3 = sb("s3", [128, 2, W])
        p3 = sb("p3", [128, 2, W])
        l3 = sb("l3", [128, 2, HALF * H])
        pT3 = sb("pT3", [128, 2, W])
        o3 = sb("o3", [128, 2, W])
        oT3 = sb("oT3", [128, 2, W])
        n4 = sb("n4", [128, 2, W])
        nT4 = sb("nT4", [128, 2, W])
        lg = sb("lg", [128, B, NR])
        top8 = sb("top8", [128, B, 8])
        top2 = sb("top2", [128, B, 8])
        rest = sb("rest", [128, B, NE])
        chosen = sb("chosen", [128, B, NE])
        le = sb("le", [128, B, NR])
        ex = sb("ex", [128, B, NR])
        exc = sb("exc", [128, B, NR])
        den = sb("den", [128, B, 2])
        rden = sb("rden", [128, B, 2])
        wt = sb("wt", [128, B, NR])
        whi = sb("whi", [128, B, 3, NR], BF16)
        wr1 = sb("wr1", [128, B, NR])
        wr2 = sb("wr2", [128, B, NR])
        wT = sb("wT", [3 * NR, B * S], BF16)
        e_sil = sb("e_sil", [128, 2, W])
        e_t = sb("e_t", [128, 2, W])
        e_h = sb("e_h", [128, 2, W])

        names = """ld_x ld_c ld_a ld_r ld_f ld_l ld_s ld_e stored ident_ok const_ok gates_ok v_proj v_ok
            ln_stats ln_mv ln_ve ln_rstd
            a_xn a_xT a_xTs a_K a_ks a_Q a_qs a_S a_mx a_sub a_exp a_T a_Ts a_PV a_rl a_on a_OT a_OTs a_y a_res
            w_abs w_sum w_mean w_clip w_scale w_deq w_r32 w_clipd w_q
            f_xstep f_xqr f_xqTp f_xqTs f_gp f_up f_silr f_hr f_hstep f_htr f_hqr f_hTp f_hTs f_yp f_res
            k3p k3s v3p v3s n3r t3p t3s q3p q3s s3p m3r s3r p3r l3r r3r pt3p pt3s o3p o3r ot3p ot3s y3p x3r
            n4r t4p t4s lgp lgs r_top r_two r_rest r_chosen r_le r_ex r_exc r_den r_rden r_wt r_split wTp wTs
            e_Gp e_gp e_up e_silr e_tr e_hr e_yp e_res""".split()
        sm = {n: sem(n) for n in names}
        block = es.enter_context(nc.Block())

        def tok(t, n, w=128):
            return t[:, bass.ts(n, w)]

        STEPS1 = 6
        STEPS2 = 5

        @block.sync
        def _(sp):
            sp.dma_start(x_all[:, :], x).then_inc(sm["ld_x"], 16)
            sp.dma_start(a[:, :], aw).then_inc(sm["ld_a"], 16)
            sp.dma_start(fws[:, :], fw).then_inc(sm["ld_f"], 16)
            sp.dma_start(ews[:, :], ew).then_inc(sm["ld_e"], 16)
            for s in range(2):
                sp.wait_ge(sm["e_res"], s + 1)
                sp.dma_start(out[:, s * W:(s + 1) * W], x_all[:, s * W:(s + 1) * W]).then_inc(sm["stored"], 16)
            sp.wait_ge(sm["stored"], 32)

        @block.gpsimd
        def _(pool):
            nc.gpsimd.memset(identb[:, :], 0.0).then_inc(sm["ident_ok"], 1)
            nc.gpsimd.memset(maskb[:, :], 0.0).then_inc(sm["ident_ok"], 1)
            pool.wait_ge(sm["ident_ok"], 2)
            nc.gpsimd.affine_select(out=identb[:, :], in_=identb[:, :], compare_op=ALU.not_equal, fill=1.0,
                                    base=0, pattern=[[-1, 128]], channel_multiplier=1).then_inc(sm["ident_ok"], 1)
            nc.gpsimd.affine_select(out=maskb[:, :], in_=maskb[:, :], compare_op=ALU.is_ge, fill=MASKED,
                                    base=0, pattern=[[-1, 128]], channel_multiplier=1).then_inc(sm["ident_ok"], 1)
            nc.gpsimd.memset(ones_row[:, :], 1.0).then_inc(sm["const_ok"], 1)
            nc.gpsimd.memset(ones_sq[:, :], 1.0).then_inc(sm["const_ok"], 1)
            nc.gpsimd.memset(mhalf[:, :], -0.5).then_inc(sm["const_ok"], 1)
            nc.gpsimd.memset(top2[:, :, :], 3e38).then_inc(sm["const_ok"], 1)
            pool.wait_ge(sm["const_ok"], 4)

            def rstd_of(r):
                pool.wait_ge(sm["ln_mv"], 8 * (r + 1))
                nc.gpsimd.tensor_scalar(ve[:, :], mv[:, :].rearrange("p (b t) -> p b t", t=2)[:, :, 1], EPS, None,
                                        ALU.add).then_inc(sm["ln_ve"], 1)
                pool.wait_ge(sm["ln_ve"], r + 1)
                nc.gpsimd.tensor_tensor(rstd[:, :], ve[:, :], mhalf[:, :], ALU.pow).then_inc(sm["ln_rstd"], 1)

            rstd_of(0)
            pool.wait_ge(sm["w_scale"], 1)
            for m in range(3):
                nc.gpsimd.tensor_scalar(fq32[:, bass.ts(m, INNER)], fws[:, bass.ts(m, INNER)], fscale[:, m:m + 1],
                                        MAGIC, ALU.mult, ALU.add).then_inc(sm["w_r32"], 1)
            for m in range(3):
                pool.wait_ge(sm["w_r32"], m + 1)
                nc.gpsimd.tensor_scalar(fqc[:, bass.ts(m, INNER)], fq32[:, bass.ts(m, INNER)], MAGIC, 1.0,
                                        ALU.subtract, ALU.min).then_inc(sm["w_clipd"], 1)
            for m in range(3):
                pool.wait_ge(sm["w_clipd"], m + 1)
                nc.gpsimd.tensor_scalar(fq[:, m, :], fqc[:, bass.ts(m, INNER)], -1.0, None,
                                        ALU.max).then_inc(sm["w_q"], 1)
            rstd_of(1)

            rstd_of(2)
            rstd_of(3)

        @block.scalar
        def _(act):
            act.dma_start(cT[:, :], ctxT).then_inc(sm["ld_c"], 16)
            act.dma_start(bo[:, :], rows).then_inc(sm["ld_r"], 16)
            act.dma_start(lws[:, :], lw).then_inc(sm["ld_l"], 16)
            act.dma_start(sels[:, :], sel).then_inc(sm["ld_s"], 16)
            act.wait_ge(sm["ld_a"], 16)
            nc.scalar.activation(tg[:, :], a[:, A_GX:A_GX + 4], ACT.Tanh).then_inc(sm["gates_ok"], 1)

            def xT_copy(n, u):
                act.wait_ge(sm["a_xT"], n + 1)
                nc.scalar.activation(xnT[:, u, :], bank[6][:, 0:S], ACT.Copy).then_inc(sm["a_xTs"], 1)

            def oT_copy(n):
                act.wait_ge(sm["a_OT"], n + 1)
                nc.scalar.activation(oT[:, :], bank[7][:, 256:384], ACT.Identity,
                                     bias=a[:, A_BV:A_BV + 1]).then_inc(sm["a_OTs"], 1)

            def attn(n, first, last, un):
                def exp(j):
                    act.wait_ge(sm["a_sub"], 4 * n + j + 1)
                    if not first:
                        act.wait_ge(sm["a_T"], 4 * n + j - 3)
                    nc.scalar.activation(pr[:, j, :], sx[:, j, :], ACT.Exp, scale=SCALE).then_inc(sm["a_exp"], 1)

                def pT_copy(j):
                    act.wait_ge(sm["a_T"], 4 * n + j + 1)
                    if not first or j >= 2:
                        act.wait_ge(sm["a_PV"], 4 * n + j - 1)
                    nc.scalar.activation(pT[:, j % 2, :], bank[4 + j % 2][:, :], ACT.Copy).then_inc(sm["a_Ts"], 1)

                if not last:
                    xT_copy(n + 1, un)
                if not first:
                    oT_copy(n - 1)
                exp(0)
                exp(1)
                pT_copy(0)
                exp(2)
                pT_copy(1)
                exp(3)
                pT_copy(2)
                pT_copy(3)

            xT_copy(0, 0)
            attn(0, True, False, 1)
            with act.Fori(0, B // 2 - 1) as i:
                attn(2 * i + 1, False, False, 0)
                attn(2 * i + 2, False, False, 1)
            attn(B - 1, False, True, 0)
            oT_copy(B - 1)

            def xqT_copy(n, u):
                act.wait_ge(sm["f_xqTp"], n + 1)
                nc.scalar.activation(f_xqT[:, u, :], bank[0][:, :].bitcast(BF16)[:, 0:S], ACT.Copy).then_inc(sm["f_xqTs"], 1)

            def ffn(n, u, last):
                if not last:
                    xqT_copy(n + 1, 1 - u)
                act.wait_ge(sm["f_gp"], n + 1)
                act.wait_ge(sm["f_xstep"], STEPS1 * n + 4)
                nc.scalar.activation(f_sil[:, u, :], bank[1 + u][:, :], ACT.Silu,
                                     scale=f_deq[:, u, 0:1]).then_inc(sm["f_silr"], 1)
                act.wait_ge(sm["f_hstep"], STEPS2 * n + 4)
                nc.scalar.activation(f_ht[:, :], f_h[:, u, :], ACT.Identity,
                                     scale=f_ah[:, u, 2:3]).then_inc(sm["f_htr"], 1)
                act.wait_ge(sm["f_hTp"], n + 1)
                nc.scalar.activation(f_hqT[:, u, :], bank[5][:, :].bitcast(BF16)[:, 0:INNER], ACT.Copy).then_inc(sm["f_hTs"], 1)

            xqT_copy(0, 0)
            with act.Fori(0, B // 2 - 1) as i:
                ffn(2 * i, 0, False)
                ffn(2 * i + 1, 1, False)
            ffn(B - 2, 0, False)
            ffn(B - 1, 1, True)

            for s in range(2):
                act.wait_ge(sm["t3p"], s + 1)
                nc.scalar.activation(nT3[:, s, :], bank[s][:, :], ACT.Copy).then_inc(sm["t3s"], 1)
            for s in range(2):
                act.wait_ge(sm["q3p"], s + 1)
                nc.scalar.activation(q3[:, s, :], bank[s][:, :], ACT.Identity,
                                     bias=lws[:, L_BQ:L_BQ + 1]).then_inc(sm["q3s"], 1)
            for s in range(2):
                act.wait_ge(sm["s3r"], s + 1)
                nc.scalar.activation(p3[:, s, :], s3[:, s, :], ACT.Exp, scale=SCALE).then_inc(sm["p3r"], 1)
            for s in range(2):
                act.wait_ge(sm["pt3p"], s + 1)
                nc.scalar.activation(pT3[:, s, :], bank[s][:, :], ACT.Copy).then_inc(sm["pt3s"], 1)
            for s in range(2):
                act.wait_ge(sm["ot3p"], s + 1)
                nc.scalar.activation(oT3[:, s, :], bank[s][:, :], ACT.Identity,
                                     bias=lws[:, L_BV:L_BV + 1]).then_inc(sm["ot3s"], 1)

            for s in range(2):
                act.wait_ge(sm["t4p"], s + 1)
                nc.scalar.activation(nT4[:, s, :], bank[s][:, :], ACT.Copy).then_inc(sm["t4s"], 1)
            act.wait_ge(sm["lgp"], 1)
            nc.scalar.activation(lg[:, :, :], bank[4][:, 0:B * NR].rearrange("p (b e) -> p b e", e=NR),
                                 ACT.Copy).then_inc(sm["lgs"], 1)
            act.wait_ge(sm["r_le"], 2)
            nc.scalar.activation(ex[:, :, :], le[:, :, :], ACT.Exp).then_inc(sm["r_ex"], 1)
            for s in range(2):
                act.wait_ge(sm["wTp"], s + 1)
                nc.scalar.activation(wT[:, s * W:(s + 1) * W], bank[5 + s][:, :].bitcast(BF16)[0:3 * NR, 0:W],
                                     ACT.Copy).then_inc(sm["wTs"], 1)

            for k in range(2 * NC):
                act.wait_ge(sm["e_gp"], k + 1)
                if k >= 2:
                    act.wait_ge(sm["e_tr"], k - 1)
                nc.scalar.activation(e_sil[:, k % 2, :], bank[k % 2][:, :], ACT.Silu).then_inc(sm["e_silr"], 1)

        @block.vector
        def _(dve):
            V = nc.vector

            def aggregate(r):
                dve.wait_ge(sm["ln_stats"], B * (r + 1))
                for b in range(B):
                    V.bn_aggr(mv[:, 2 * b:2 * b + 2], stats[:, 6 * b:6 * b + 6]).then_inc(sm["ln_mv"], 1)
                dve.wait_ge(sm["ln_mv"], B * (r + 1))
                dve.wait_ge(sm["ln_rstd"], r + 1)

            def normalize(dst, n):
                return V.tensor_scalar(dst, tok(x_all, n), mv[:, bass.ds(2 * n, 1)], rstd[:, bass.ds(n, 1)],
                                       ALU.subtract, ALU.mult)

            dve.wait_ge(sm["ld_x"], 16)
            for b in range(B):
                V.bn_stats(stats[:, 6 * b:6 * b + 6], x_all[:, b * D:(b + 1) * D]).then_inc(sm["ln_stats"], 1)
            aggregate(0)
            normalize(xn[:, 0, :], 0).then_inc(sm["a_xn"], 1)

            va = vaug[:, :].rearrange("p (n e) -> p n e", e=VW)
            V.memset(va[:, :, DK:VW], 1.0).then_inc(sm["v_ok"], 1)
            for s in range(2):
                dve.wait_ge(sm["v_proj"], s + 1)
                V.tensor_copy(va[:, s * HALF * H:(s + 1) * HALF * H, 0:DK],
                              bank[4 + s][:, :].rearrange("p (n e) -> p n e", e=DK)).then_inc(sm["v_ok"], 1)

            def bias_bc(col):
                return a[:, col:col + NG].unsqueeze(2).to_broadcast([128, NG, S])

            def k_copy(n, u):
                dve.wait_ge(sm["a_K"], n + 1)
                V.tensor_tensor(kT[:, u, :].rearrange("p (g t) -> p g t", g=NG),
                                bank[6][:, :].rearrange("p (g t) -> p g t", g=NG), bias_bc(A_BK),
                                ALU.add).then_inc(sm["a_ks"], 1)

            def q_copy(n, u):
                dve.wait_ge(sm["a_Q"], n + 1)
                V.tensor_tensor(qT[:, u, :].rearrange("p (g t) -> p g t", g=NG),
                                bank[6][:, :].rearrange("p (g t) -> p g t", g=NG), bias_bc(A_BQ),
                                ALU.add).then_inc(sm["a_qs"], 1)

            def heads_out(n):
                o = bank[7][:, 0:H * VW].rearrange("p (h e) -> p h e", e=VW)
                dve.wait_ge(sm["a_PV"], 4 * n + 4)
                V.reciprocal(rl[:, :], o[:, :, DK]).then_inc(sm["a_rl"], 1)
                dve.wait_ge(sm["a_rl"], n + 1)
                V.tensor_tensor(on[:, :].rearrange("p (h e) -> p h e", e=DK), o[:, :, 0:DK],
                                rl[:, :].unsqueeze(2).to_broadcast([128, H, DK]), ALU.mult).then_inc(sm["a_on"], 1)

            def residual(n):
                dve.wait_ge(sm["a_y"], n + 1)
                V.scalar_tensor_tensor(tok(x_all, n), bank[7][:, 384:512], tg[:, 0:1], tok(x_all, n),
                                       ALU.mult, ALU.add).then_inc(sm["a_res"], 1)
                dve.wait_ge(sm["a_res"], n + 1)
                V.bn_stats(tok(stats, n, 6), tok(x_all, n)).then_inc(sm["ln_stats"], 1)

            def attn(n, u, first, last):
                def top(j):
                    dve.wait_ge(sm["a_S"], 4 * n + j + 1)
                    V.tensor_reduce(mx[:, u, j, :], bank[j][:, :].rearrange("p (g k) -> p g k", g=NG), AX.X,
                                    ALU.max).then_inc(sm["a_mx"], 1)

                def sub(j):
                    dve.wait_ge(sm["a_mx"], 4 * n + j + 1)
                    if not first:
                        dve.wait_ge(sm["a_exp"], 4 * n + j - 3)
                    V.tensor_tensor(sx[:, j, :].rearrange("p (g k) -> p g k", g=NG),
                                    bank[j][:, :].rearrange("p (g k) -> p g k", g=NG),
                                    mx[:, u, j, :].unsqueeze(2).to_broadcast([128, NG, S]),
                                    ALU.subtract).then_inc(sm["a_sub"], 1)

                if not last:
                    normalize(xn[:, 1 - u, :], n + 1).then_inc(sm["a_xn"], 1)
                if not first:
                    heads_out(n - 1)
                top(0)
                top(1)
                sub(0)
                if not last:
                    k_copy(n + 1, 1 - u)
                top(2)
                sub(1)
                if not first:
                    residual(n - 1)
                top(3)
                sub(2)
                sub(3)
                if not last:
                    q_copy(n + 1, 1 - u)

            dve.wait_ge(sm["ld_a"], 16)
            k_copy(0, 0)
            q_copy(0, 0)
            dve.wait_ge(sm["gates_ok"], 1)
            attn(0, 0, True, False)

            dve.wait_ge(sm["ld_f"], 16)
            V.tensor_reduce(fabs[:, :], fws[:, :].rearrange("p (m n) -> p m n", m=3), AX.X, ALU.add,
                            apply_absolute_value=True).then_inc(sm["w_abs"], 1)
            dve.wait_ge(sm["w_sum"], 1)
            V.tensor_scalar(fmean[:, :], bank[6][:, 0:3], 1.0 / (INNER * D), None, ALU.mult).then_inc(sm["w_mean"], 1)
            dve.wait_ge(sm["w_mean"], 1)
            V.tensor_scalar(fclip[:, :], fmean[:, :], QMIN, None, ALU.max).then_inc(sm["w_clip"], 1)
            dve.wait_ge(sm["w_clip"], 1)
            V.reciprocal(fscale[:, :], fclip[:, :]).then_inc(sm["w_scale"], 1)
            V.tensor_scalar(fdeq[:, 0:2], fclip[:, 0:2], 1.0 / 127.0, None, ALU.mult).then_inc(sm["w_deq"], 1)
            V.tensor_scalar(fdeq[:, 2:3], fclip[:, 2:3], 1.0 / 127.0, tg[:, 2:3], ALU.mult, ALU.mult)\
                .then_inc(sm["w_deq"], 1)
            with dve.Fori(0, B // 2 - 1) as i:
                attn(2 * i + 1, 1, False, False)
                attn(2 * i + 2, 0, False, False)
            attn(B - 1, 1, False, True)
            heads_out(B - 1)

            dve.wait_ge(sm["ld_l"], 16)
            for s in range(2):
                dve.wait_ge(sm["k3p"], s + 1)
                V.scalar_tensor_tensor(kb[:, s, :].rearrange("p (b t) -> p b t", b=HALF),
                                       bank[s][:, :].rearrange("p (b t) -> p b t", b=HALF), lws[:, L_BK:L_BK + 1],
                                       lws[:, L_MK:L_MK + S].unsqueeze(1).to_broadcast([128, HALF, S]),
                                       ALU.add, ALU.mult).then_inc(sm["k3s"], 1)
                dve.wait_ge(sm["v3p"], s + 1)
                V.tensor_tensor(vb[:, s, :].rearrange("p (b t) -> p b t", b=HALF),
                                bank[2 + s][:, :].rearrange("p (b t) -> p b t", b=HALF),
                                lws[:, L_MV:L_MV + D].unsqueeze(1).to_broadcast([128, HALF, D]),
                                ALU.mult).then_inc(sm["v3s"], 1)
            residual(B - 1)

            aggregate(1)

            def x_quant(n, u):
                at = lambda k: STEPS1 * n + k
                normalize(f_xn[:, :], n).then_inc(sm["f_xstep"], 1)
                dve.wait_ge(sm["f_xstep"], at(1))
                V.tensor_reduce(f_a[:, 0:1], f_xn[:, :], AX.X, ALU.max,
                                apply_absolute_value=True).then_inc(sm["f_xstep"], 1)
                dve.wait_ge(sm["f_xstep"], at(2))
                V.tensor_scalar(f_a[:, 1:2], f_a[:, 0:1], QMIN, None, ALU.max).then_inc(sm["f_xstep"], 1)
                dve.wait_ge(sm["f_xstep"], at(3))
                V.tensor_scalar(f_deq[:, u, :], fdeq[:, 0:2], f_a[:, 1:2], None, ALU.mult).then_inc(sm["f_xstep"], 1)
                V.reciprocal(f_a[:, 2:3], f_a[:, 1:2]).then_inc(sm["f_xstep"], 1)
                dve.wait_ge(sm["f_xstep"], at(5))
                V.tensor_scalar(f_t[:, :], f_xn[:, :], f_a[:, 2:3], 127.0, ALU.mult, ALU.mult).then_inc(sm["f_xstep"], 1)
                dve.wait_ge(sm["f_xstep"], at(6))
                V.tensor_scalar(f_xq[:, u, :], f_t[:, :], MAGIC, MAGIC, ALU.add, ALU.subtract).then_inc(sm["f_xqr"], 1)

            def ffn_residual(n, u):
                dve.wait_ge(sm["f_yp"], n + 1)
                V.scalar_tensor_tensor(tok(x_all, n), bank[6][:, 0:D], f_ah[:, u, 3:4], tok(x_all, n),
                                       ALU.mult, ALU.add).then_inc(sm["f_res"], 1)
                dve.wait_ge(sm["f_res"], n + 1)
                V.bn_stats(tok(stats, n, 6), tok(x_all, n)).then_inc(sm["ln_stats"], 1)

            def ffn(n, u, first, last):
                at = lambda k: STEPS2 * n + k
                if not last:
                    x_quant(n + 1, 1 - u)
                dve.wait_ge(sm["f_up"], n + 1)
                dve.wait_ge(sm["f_silr"], n + 1)
                V.scalar_tensor_tensor(f_h[:, u, :], bank[3 + u][:, :], f_deq[:, u, 1:2], f_sil[:, u, :],
                                       ALU.mult, ALU.mult).then_inc(sm["f_hr"], 1)
                dve.wait_ge(sm["f_hr"], n + 1)
                V.tensor_reduce(f_ah[:, u, 0:1], f_h[:, u, :], AX.X, ALU.max,
                                apply_absolute_value=True).then_inc(sm["f_hstep"], 1)
                dve.wait_ge(sm["f_hstep"], at(1))
                V.tensor_scalar(f_ah[:, u, 1:2], f_ah[:, u, 0:1], QMIN, None, ALU.max).then_inc(sm["f_hstep"], 1)
                dve.wait_ge(sm["f_hstep"], at(2))
                V.reciprocal(f_ah[:, u, 4:5], f_ah[:, u, 1:2]).then_inc(sm["f_hstep"], 1)
                dve.wait_ge(sm["f_hstep"], at(3))
                V.tensor_scalar(f_ah[:, u, 2:3], f_ah[:, u, 4:5], 127.0, None, ALU.mult).then_inc(sm["f_hstep"], 1)
                V.tensor_scalar(f_ah[:, u, 3:4], f_ah[:, u, 1:2], fdeq[:, 2:3], None, ALU.mult).then_inc(sm["f_hstep"], 1)
                if not first:
                    ffn_residual(n - 1, 1 - u)
                dve.wait_ge(sm["f_htr"], n + 1)
                V.tensor_scalar(f_hq[:, u, :], f_ht[:, :], MAGIC, MAGIC, ALU.add, ALU.subtract).then_inc(sm["f_hqr"], 1)

            dve.wait_ge(sm["w_deq"], 2)
            x_quant(0, 0)
            ffn(0, 0, True, False)
            with dve.Fori(0, B // 2 - 1) as i:
                ffn(2 * i + 1, 1, False, False)
                ffn(2 * i + 2, 0, False, False)
            ffn(B - 1, 1, False, True)
            dve.wait_ge(sm["f_hstep"], STEPS2 * B)
            ffn_residual(B - 1, 1)

            aggregate(2)
            for s in range(2):
                for b in range(HALF):
                    last = normalize(n3[:, s, b * D:(b + 1) * D], HALF * s + b)
                last.then_inc(sm["n3r"], 1)
            for s in range(2):
                dve.wait_ge(sm["s3p"], s + 1)
                sc = bank[2 + s][:, :].rearrange("p (b j h) -> p b h j", b=HALF, h=H)
                V.tensor_reduce(m3[:, s, :].rearrange("p (b h) -> p b h", h=H), sc, AX.X, ALU.max).then_inc(sm["m3r"], 1)
            for s in range(2):
                dve.wait_ge(sm["m3r"], s + 1)
                V.tensor_tensor(s3[:, s, :].rearrange("p (b j h) -> p b j h", b=HALF, h=H),
                                bank[2 + s][:, :].rearrange("p (b j h) -> p b j h", b=HALF, h=H),
                                m3[:, s, :].rearrange("p (b h) -> p b h", h=H).unsqueeze(2)
                                .to_broadcast([128, HALF, KEYS, H]), ALU.subtract).then_inc(sm["s3r"], 1)
            for s in range(2):
                dve.wait_ge(sm["p3r"], s + 1)
                V.tensor_reduce(m3[:, s, :].rearrange("p (b h) -> p b h", h=H),
                                p3[:, s, :].rearrange("p (b j h) -> p b h j", b=HALF, h=H), AX.X,
                                ALU.add).then_inc(sm["l3r"], 1)
            for s in range(2):
                dve.wait_ge(sm["l3r"], s + 1)
                V.reciprocal(l3[:, s, :], m3[:, s, :]).then_inc(sm["r3r"], 1)
            for s in range(2):
                dve.wait_ge(sm["o3p"], s + 1)
                dve.wait_ge(sm["r3r"], s + 1)
                V.tensor_tensor(o3[:, s, :].rearrange("p (n e) -> p n e", e=DK),
                                bank[4 + s][:, :].rearrange("p (n e) -> p n e", e=DK),
                                l3[:, s, :].unsqueeze(2).to_broadcast([128, HALF * H, DK]),
                                ALU.mult).then_inc(sm["o3r"], 1)
            for s in range(2):
                dve.wait_ge(sm["y3p"], s + 1)
                xs = x_all[:, s * W:(s + 1) * W]
                V.scalar_tensor_tensor(xs, bank[6 + s][:, :], tg[:, 1:2], xs, ALU.mult, ALU.add).then_inc(sm["x3r"], 1)
            for b in range(B):
                dve.wait_ge(sm["x3r"], b // HALF + 1)
                V.bn_stats(stats[:, 6 * b:6 * b + 6], x_all[:, b * D:(b + 1) * D]).then_inc(sm["ln_stats"], 1)

            aggregate(3)
            for s in range(2):
                for b in range(HALF):
                    last = normalize(n4[:, s, b * D:(b + 1) * D], HALF * s + b)
                last.then_inc(sm["n4r"], 1)
            dve.wait_ge(sm["const_ok"], 4)
            dve.wait_ge(sm["lgs"], 1)
            for b in range(B):
                V.max(top8[:, b, :], lg[:, b, 0:NE]).then_inc(sm["r_top"], 1)
            dve.wait_ge(sm["r_top"], B)
            V.tensor_copy(top2[:, :, 0:2], top8[:, :, 0:2]).then_inc(sm["r_two"], 1)
            V.tensor_tensor(le[:, :, 0:NE], lg[:, :, 0:NE], top8[:, :, 0:1].to_broadcast([128, B, NE]),
                            ALU.subtract).then_inc(sm["r_le"], 1)
            V.tensor_scalar(le[:, :, NE:NR], lg[:, :, NE:NR], -1.0, None, ALU.mult).then_inc(sm["r_le"], 1)
            dve.wait_ge(sm["r_two"], 1)
            for b in range(B):
                V.match_replace(rest[:, b, :], top2[:, b, :], lg[:, b, 0:NE], MASKED).then_inc(sm["r_rest"], 1)
            dve.wait_ge(sm["r_rest"], B)
            V.tensor_tensor(chosen[:, :, :], rest[:, :, :], lg[:, :, 0:NE], ALU.not_equal).then_inc(sm["r_chosen"], 1)
            dve.wait_ge(sm["r_chosen"], 1)
            dve.wait_ge(sm["r_ex"], 1)
            V.tensor_tensor(exc[:, :, 0:NE], ex[:, :, 0:NE], chosen[:, :, :], ALU.mult).then_inc(sm["r_exc"], 1)
            V.tensor_scalar(den[:, :, 1:2], ex[:, :, NE:NR], 1.0, None, ALU.add).then_inc(sm["r_den"], 1)
            V.memset(exc[:, :, NE:NR], 1.0).then_inc(sm["r_exc"], 1)
            dve.wait_ge(sm["r_exc"], 2)
            V.tensor_reduce(den[:, :, 0:1], exc[:, :, 0:NE], AX.X, ALU.add).then_inc(sm["r_den"], 1)
            dve.wait_ge(sm["r_den"], 2)
            V.reciprocal(rden[:, :, :], den[:, :, :]).then_inc(sm["r_rden"], 1)
            dve.wait_ge(sm["r_rden"], 1)
            V.tensor_tensor(wt[:, :, 0:NE], exc[:, :, 0:NE], rden[:, :, 0:1].to_broadcast([128, B, NE]),
                            ALU.mult).then_inc(sm["r_wt"], 1)
            V.tensor_tensor(wt[:, :, NE:NR], exc[:, :, NE:NR], rden[:, :, 1:2], ALU.mult).then_inc(sm["r_wt"], 1)
            dve.wait_ge(sm["r_wt"], 2)
            V.tensor_copy(whi[:, :, 0, :], wt[:, :, :]).then_inc(sm["r_split"], 1)
            dve.wait_ge(sm["r_split"], 1)
            V.tensor_tensor(wr1[:, :, :], wt[:, :, :], whi[:, :, 0, :], ALU.subtract).then_inc(sm["r_split"], 1)
            dve.wait_ge(sm["r_split"], 2)
            V.tensor_copy(whi[:, :, 1, :], wr1[:, :, :]).then_inc(sm["r_split"], 1)
            dve.wait_ge(sm["r_split"], 3)
            V.tensor_tensor(whi[:, :, 2, :], wr1[:, :, :], whi[:, :, 1, :], ALU.subtract).then_inc(sm["r_split"], 1)

            for k in range(2 * NC):
                s, c, u = k // NC, k % NC, k % 2
                dve.wait_ge(sm["e_silr"], k + 1)
                dve.wait_ge(sm["e_up"], k + 1)
                V.tensor_tensor(e_t[:, u, :], e_sil[:, u, :], bank[2 + u][:, :], ALU.mult).then_inc(sm["e_tr"], 1)
                dve.wait_ge(sm["e_tr"], k + 1)
                dve.wait_ge(sm["e_Gp"], k + 1)
                if k >= 2:
                    dve.wait_ge(sm["e_yp"], k - 1)
                V.tensor_tensor(e_h[:, u, :], e_t[:, u, :], bank[4 + u][:, :], ALU.mult).then_inc(sm["e_hr"], 1)
                if c == NC - 1:
                    dve.wait_ge(sm["e_yp"], k + 1)
                    xs = x_all[:, s * W:(s + 1) * W]
                    V.scalar_tensor_tensor(xs, bank[6 + s][:, :], tg[:, 3:4], xs, ALU.mult, ALU.add)\
                        .then_inc(sm["e_res"], 1)

        @block.tensor
        def _(pe):
            mm = nc.tensor.matmul
            pe.wait_ge(sm["ld_a"], 16)
            pe.wait_ge(sm["ld_c"], 16)
            pe.wait_ge(sm["const_ok"], 4)
            for s in range(2):
                for b in range(HALF):
                    last = mm(bank[4 + s][:, b * D:(b + 1) * D], cT[:, (HALF * s + b) * S:(HALF * s + b + 1) * S],
                              a[:, A_WV:A_WV + D], start=True, stop=True)
                last.then_inc(sm["v_proj"], 1)

            def xT(n, u):
                pe.wait_ge(sm["a_xn"], n + 1)
                nc.tensor.transpose(bank[6][:, 0:S], xn[:, u, :], ident).then_inc(sm["a_xT"], 1)

            def k_proj(n):
                pe.wait_ge(sm["a_xTs"], n + 1)
                for g in range(NG):
                    last = mm(bank[6][:, g * S:(g + 1) * S], a[:, A_WK + 128 * g:A_WK + 128 * (g + 1)], tok(cT, n),
                              start=True, stop=True)
                last.then_inc(sm["a_K"], 1)

            def q_proj(n, u):
                pe.wait_ge(sm["a_ks"], n + 1)
                for g in range(NG):
                    last = mm(bank[6][:, g * S:(g + 1) * S], a[:, A_WQ + 128 * g:A_WQ + 128 * (g + 1)], xnT[:, u, :],
                              start=True, stop=True)
                last.then_inc(sm["a_Q"], 1)

            def oT_heads(n):
                pe.wait_ge(sm["a_on"], n + 1)
                nc.tensor.transpose(bank[7][:, 256:384], on[:, :], ident).then_inc(sm["a_OT"], 1)

            def y_proj(n):
                pe.wait_ge(sm["a_OTs"], n + 1)
                mm(bank[7][:, 384:512], ones_row[:, :], bo[:, 0:D], start=True, stop=False)
                mm(bank[7][:, 384:512], oT[:, :], a[:, A_WO:A_WO + D], start=False, stop=True).then_inc(sm["a_y"], 1)

            def attn(n, u, first, last):
                pe.wait_ge(sm["a_qs"], n + 1)
                if not first:
                    pe.wait_ge(sm["a_sub"], 4 * n)
                for j in range(NQ):
                    mm(bank[j][:, :], identb[:, :], maskb[:, :].unsqueeze(1).to_broadcast([128, NG, S]),
                       start=True, stop=False)
                for g in range(NG):
                    for j in range(NQ):
                        rows = slice(QW * j, QW * (j + 1))
                        ins = mm(bank[j][:, g * S:(g + 1) * S], qT[rows, u, g * S:(g + 1) * S],
                                 kT[rows, u, g * S:(g + 1) * S], start=False, stop=(g == NG - 1))
                        if g == NG - 1:
                            ins.then_inc(sm["a_S"], 1)
                if not last:
                    xT(n + 1, 1 - u)
                if not first:
                    oT_heads(n - 1)
                if not last:
                    k_proj(n + 1)
                if not first:
                    y_proj(n - 1)

                def transposes(j):
                    pe.wait_ge(sm["a_exp"], 4 * n + j + 1)
                    if not first or j >= 2:
                        pe.wait_ge(sm["a_Ts"], 4 * n + j - 1)
                    for g in range(NG):
                        last = nc.tensor.transpose(bank[4 + j % 2][:, g * S:(g + 1) * S],
                                                   pr[:, j, g * S:(g + 1) * S], ident)
                    last.then_inc(sm["a_T"], 1)

                def pv(j):
                    pe.wait_ge(sm["a_Ts"], 4 * n + j + 1)
                    if j == 0 and not first:
                        pe.wait_ge(sm["a_res"], n)
                    for g in range(NG):
                        h = NQ * g + j
                        last = mm(bank[7][:, h * VW:(h + 1) * VW], pT[:, j % 2, g * S:(g + 1) * S],
                                  vaug[:, bass.ds(n * (H * VW) + h * VW, VW)], start=True, stop=True)
                    last.then_inc(sm["a_PV"], 1)

                transposes(0)
                transposes(1)
                pv(0)
                if not last:
                    q_proj(n + 1, 1 - u)
                transposes(2)
                pv(1)
                transposes(3)
                pv(2)
                pv(3)

            pe.wait_ge(sm["ident_ok"], 4)
            xT(0, 0)
            k_proj(0)
            q_proj(0, 0)
            pe.wait_ge(sm["v_ok"], 3)
            pe.wait_ge(sm["ld_r"], 16)
            attn(0, 0, True, False)
            pe.wait_ge(sm["a_qs"], 2)
            pe.wait_ge(sm["w_abs"], 1)
            mm(bank[6][:, 0:3], ones_sq[:, :], fabs[:, :], start=True, stop=True).then_inc(sm["w_sum"], 1)
            pe.wait_ge(sm["w_mean"], 1)
            with pe.Fori(0, B // 2 - 1) as i:
                attn(2 * i + 1, 1, False, False)
                attn(2 * i + 2, 0, False, False)
            attn(B - 1, 1, False, True)
            pe.wait_ge(sm["a_sub"], 4 * B)
            pe.wait_ge(sm["ld_l"], 16)
            for s in range(2):
                mm(bank[s][:, :], lws[:, L_WK:L_WK + D], cT[:, s * W:(s + 1) * W],
                   start=True, stop=True).then_inc(sm["k3p"], 1)
                for b in range(HALF):
                    n = HALF * s + b
                    last = mm(bank[2 + s][:, b * D:(b + 1) * D], cT[:, n * S:(n + 1) * S], lws[:, L_WV:L_WV + D],
                              start=True, stop=True)
                last.then_inc(sm["v3p"], 1)
            oT_heads(B - 1)
            y_proj(B - 1)

            def x_part(n, u, first):
                pe.wait_ge(sm["f_xqr"], n + 1)
                if not first:
                    pe.wait_ge(sm["f_xqTs"], n)
                nc.tensor.transpose(bank[0][:, :].bitcast(BF16)[:, 0:S], f_xq[:, u, :], identb[:, :]).then_inc(sm["f_xqTp"], 1)

            def gate_up(n, u, first):
                pe.wait_ge(sm["f_xqTs"], n + 1)
                if not first:
                    pe.wait_ge(sm["f_silr"], n - 1)
                    pe.wait_ge(sm["f_hr"], n - 1)
                mm(bank[1 + u][:, :], f_xqT[:, u, :], fq[:, 0, :], start=True, stop=True).then_inc(sm["f_gp"], 1)
                mm(bank[3 + u][:, :], f_xqT[:, u, :], fq[:, 1, :], start=True, stop=True).then_inc(sm["f_up"], 1)

            def down(n, u, first):
                pe.wait_ge(sm["f_hqr"], n + 1)
                if not first:
                    pe.wait_ge(sm["f_hTs"], n)
                for c in range(4):
                    last = nc.tensor.transpose(bank[5][:, :].bitcast(BF16)[:, c * S:(c + 1) * S],
                                               f_hq[:, u, c * 128:(c + 1) * 128], identb[:, :])
                last.then_inc(sm["f_hTp"], 1)
                pe.wait_ge(sm["f_hTs"], n + 1)
                if not first:
                    pe.wait_ge(sm["f_res"], n)
                for c in range(4):
                    last = mm(bank[6][:, 0:D], f_hqT[:, u, c * S:(c + 1) * S], fq[:, 2, c * D:(c + 1) * D],
                              start=(c == 0), stop=(c == 3))
                last.then_inc(sm["f_yp"], 1)

            pe.wait_ge(sm["w_q"], 3)
            x_part(0, 0, True)
            gate_up(0, 0, True)
            x_part(1, 1, False)
            gate_up(1, 1, True)
            down(0, 0, True)
            with pe.Fori(0, B // 2 - 1) as i:
                x_part(2 * i + 2, 0, False)
                gate_up(2 * i + 2, 0, False)
                down(2 * i + 1, 1, False)
                x_part(2 * i + 3, 1, False)
                gate_up(2 * i + 3, 1, False)
                down(2 * i + 2, 0, False)
            down(B - 1, 1, False)

            hb = lambda s, b: slice((HALF * s + b) * S, (HALF * s + b + 1) * S)
            pe.wait_ge(sm["k3s"], 2)
            pe.wait_ge(sm["v3s"], 2)
            pe.wait_ge(sm["f_res"], B)
            for s in range(2):
                pe.wait_ge(sm["n3r"], s + 1)
                for b in range(HALF):
                    last = nc.tensor.transpose(bank[s][:, b * S:(b + 1) * S], n3[:, s, b * D:(b + 1) * D], ident)
                last.then_inc(sm["t3p"], 1)
            for s in range(2):
                pe.wait_ge(sm["t3s"], s + 1)
                mm(bank[s][:, :], lws[:, L_WQ:L_WQ + D], nT3[:, s, :], start=True, stop=True).then_inc(sm["q3p"], 1)
            for s in range(2):
                pe.wait_ge(sm["q3s"], s + 1)
                for b in range(HALF):
                    last = mm(bank[2 + s][:, b * S:(b + 1) * S], q3[:, s, b * S:(b + 1) * S],
                              kb[:, s, b * S:(b + 1) * S], start=True, stop=True)
                last.then_inc(sm["s3p"], 1)
            for s in range(2):
                pe.wait_ge(sm["p3r"], s + 1)
                for b in range(HALF):
                    last = nc.tensor.transpose(bank[s][:, b * S:(b + 1) * S], p3[:, s, b * S:(b + 1) * S], ident)
                last.then_inc(sm["pt3p"], 1)
            for s in range(2):
                pe.wait_ge(sm["pt3s"], s + 1)
                for b in range(HALF):
                    last = mm(bank[4 + s][:, b * S:(b + 1) * S], pT3[:, s, b * S:(b + 1) * S],
                              vb[:, s, b * S:(b + 1) * S], start=True, stop=True)
                last.then_inc(sm["o3p"], 1)
            for s in range(2):
                pe.wait_ge(sm["o3r"], s + 1)
                for b in range(HALF):
                    last = nc.tensor.transpose(bank[s][:, b * S:(b + 1) * S], o3[:, s, b * D:(b + 1) * D], ident)
                last.then_inc(sm["ot3p"], 1)
            for s in range(2):
                pe.wait_ge(sm["ot3s"], s + 1)
                mm(bank[6 + s][:, :], ones_row[:, :], bo[:, D:2 * D].unsqueeze(1).to_broadcast([1, HALF, D]),
                   start=True, stop=False)
                for b in range(HALF):
                    last = mm(bank[6 + s][:, b * D:(b + 1) * D], oT3[:, s, b * S:(b + 1) * S], lws[:, L_WO:L_WO + D],
                              start=False, stop=(b == HALF - 1))
                last.then_inc(sm["y3p"], 1)

            for s in range(2):
                pe.wait_ge(sm["n4r"], s + 1)
                for b in range(HALF):
                    last = nc.tensor.transpose(bank[s][:, b * S:(b + 1) * S], n4[:, s, b * D:(b + 1) * D], ident)
                last.then_inc(sm["t4p"], 1)
            for s in range(2):
                pe.wait_ge(sm["ld_e"], 16)
                pe.wait_ge(sm["t4s"], s + 1)
                for b in range(HALF):
                    n = HALF * s + b
                    last = mm(bank[4][:, n * NR:(n + 1) * NR], nT4[:, s, b * S:(b + 1) * S],
                              ews[:, NC * 3 * 128:NC * 3 * 128 + NR], start=True, stop=True)
            last.then_inc(sm["lgp"], 1)
            pe.wait_ge(sm["r_split"], 4)
            for s in range(2):
                for b in range(HALF):
                    last = nc.tensor.transpose(bank[5 + s][:, :].bitcast(BF16)[0:3 * NR, b * S:(b + 1) * S],
                                               whi[:, HALF * s + b, :, :].rearrange("p t e -> p (t e)"), identb[:, :])
                last.then_inc(sm["wTp"], 1)

            def project(k):
                s, c, u = k // NC, k % NC, k % 2
                if k >= 2:
                    pe.wait_ge(sm["e_silr"], k - 1)
                wg, wu, _ = expert(c)
                mm(bank[u][:, :], wg, nT4[:, s, :], start=True, stop=True).then_inc(sm["e_gp"], 1)
                if k >= 2:
                    pe.wait_ge(sm["e_tr"], k - 1)
                mm(bank[2 + u][:, :], wu, nT4[:, s, :], start=True, stop=True).then_inc(sm["e_up"], 1)
                if k >= 2:
                    pe.wait_ge(sm["e_hr"], k - 1)
                mm(bank[4 + u][:, :], sels[:, c * 128:(c + 1) * 128], wT[:, s * W:(s + 1) * W],
                   start=True, stop=True).then_inc(sm["e_Gp"], 1)

            def expert(c):
                return [ews[:, (3 * c + m) * 128:(3 * c + m + 1) * 128] for m in range(3)]

            pe.wait_ge(sm["wTs"], 2)
            pe.wait_ge(sm["ld_s"], 16)
            pe.wait_ge(sm["x3r"], 2)
            project(0)
            for k in range(2 * NC):
                s, c, u = k // NC, k % NC, k % 2
                if k + 1 < 2 * NC:
                    project(k + 1)
                pe.wait_ge(sm["e_hr"], k + 1)
                for b in range(HALF):
                    last = mm(bank[6 + s][:, b * D:(b + 1) * D], e_h[:, u, b * S:(b + 1) * S], expert(c)[2],
                              start=(c == 0 and b == 0), stop=(c == NC - 1), skip_group_check=True)
                last.then_inc(sm["e_yp"], 1)


def kernel(**inputs):
    import concourse.bacc as bacc
    import ml_dtypes
    from concourse.bass_utils import run_bass_kernel_spmd

    i = {k: np.asarray(v) for k, v in inputs.items()}
    f32 = np.float32

    def heads_padded(w):
        t = w.T.reshape(D, NG, NQ, DK)
        return np.pad(t, ((0, 0), (0, 0), (0, 0), (0, QW - DK))).reshape(D, NG * 128)

    def bias_padded(b):
        t = np.pad(b.reshape(NG, NQ, DK), ((0, 0), (0, 0), (0, QW - DK)))
        return t.reshape(NG, 128).T

    def all_rows(v):
        return np.broadcast_to(v.reshape(1, -1), (128, v.size))

    def chunks(w):
        return w.reshape(-1, 128, D).transpose(2, 0, 1)

    def down_chunks(w):
        return w.T.reshape(-1, 128, D).transpose(1, 0, 2)

    x = i["x"].transpose(1, 0, 2).reshape(S, B * D)
    ctxT = i["ctx_1024"].transpose(2, 0, 1).reshape(D, B * S)
    aw = np.concatenate([
        heads_padded(i["L0_xattn_w_q"]), heads_padded(i["L0_xattn_w_k"]), i["L0_xattn_w_v"].T, i["L0_xattn_w_o"].T,
        np.eye(128, dtype=f32), bias_padded(i["L0_xattn_b_q"]), bias_padded(i["L0_xattn_b_k"]),
        i["L0_xattn_b_v"].reshape(D, 1), all_rows(i["g_xattn"]), all_rows(i["g_ffn"])], axis=1)
    rows = np.concatenate([i["L0_xattn_b_o"], i["L1_xattn_bo"]]).reshape(1, 2 * D)
    fw = np.concatenate([i["L0_ffn_w_gate"].T, i["L0_ffn_w_up"].T,
                         down_chunks(i["L0_ffn_w_down"]).reshape(128, INNER)], axis=1)
    sees = (np.arange(S)[:, None] % H == np.arange(D)[None, :] // DK).astype(f32)
    lw = np.concatenate([i["L1_xattn_Wq"].T, i["L1_xattn_Wk"].T, i["L1_xattn_Wv"].T, i["L1_xattn_Wo"].T,
                         sees.T, sees, i["L1_xattn_bq"].reshape(D, 1), i["L1_xattn_bk"].reshape(D, 1),
                         i["L1_xattn_bv"].reshape(D, 1)], axis=1)
    owner = np.minimum(np.arange(NC * 128) // HID, NE)
    sel = np.tile((np.arange(NR)[:, None] == owner[None, :]), (3, 1)).astype(ml_dtypes.bfloat16)
    gate = chunks(np.concatenate([i["L1_ffn_We_gate"].reshape(NE * HID, D), i["L1_ffn_Ws_gate"]]))
    up = chunks(np.concatenate([i["L1_ffn_We_up"].reshape(NE * HID, D), i["L1_ffn_Ws_up"]]))
    down = down_chunks(np.concatenate([i["L1_ffn_We_down"].transpose(1, 0, 2).reshape(D, NE * HID),
                                       i["L1_ffn_Ws_down"]], axis=1))
    ew = np.concatenate([np.stack([gate, up, down], axis=2).reshape(128, NC * 3 * 128),
                         i["L1_ffn_Wg"].T, i["L1_ffn_Wsg"].T], axis=1)

    nc = bacc.Bacc("TRN2", target_bir_lowering=False, num_devices=1)
    arrays = dict(x=x, ctxT=ctxT, aw=aw, rows=rows, fw=fw, lw=lw, sel=sel, ew=ew)
    arrays = {f"in_{k}": np.ascontiguousarray(v) for k, v in arrays.items()}
    args = {k[3:]: nc.dram_tensor(k, v.shape, mybir.dt.from_np(v.dtype), kind="ExternalInput").ap()
            for k, v in arrays.items()}
    out = nc.dram_tensor("out_x", (S, B * D), F32, kind="ExternalOutput").ap()
    build(nc, out=out, **args)
    r = run_bass_kernel_spmd(nc, [arrays], core_ids=[0])
    return np.asarray(r.results[0]["out_x"]).reshape(S, B, D).transpose(1, 0, 2)
```

```python
from contextlib import ExitStack

import numpy as np

import concourse.bass as bass
from concourse import mybir

F32 = mybir.dt.float32
BF16 = mybir.dt.bfloat16
ALU = mybir.AluOpType
ACT = mybir.ActivationFunctionType
AX = mybir.AxisListType

B, S, D = 8, 128, 128
H, DK = 16, 8
NG, NJ = 8, 2
Q_PART = (0, 0, 1, 0, 2, 1, 1, 2)
K_PART = (0, 1, 0, 2, 0, 1, 2, 1)
NB = 4
VH = 8 * 128
DIAG = 128 + DK
INNER = 512
KEYS = 8
HALF = 4
NE, HID, SHARED = 16, 64, 256
NR = NE + 1
NC = (NE * HID + SHARED) // 128
SCALE = float(DK) ** -0.5
EPS = 1e-5
QMIN = 1e-5
MAGIC = 1.5 * 2.0 ** 23
MASKED = -1e30

A_WQ, A_WK, A_WV, A_WO, A_ID, A_BO, A_BV = (128 * k for k in range(7))
A_BQ, A_BK, A_GX, A_GF = 896, 897, 898, 900
A_COLS = 902
L_WQ, L_WK, L_WV, L_WO, L_MK, L_MV = (128 * k for k in range(6))
L_BQ, L_BK, L_BV = 768, 769, 770
L_COLS = 771


def build(nc, x, ctxT, aw, rows, fw, lw, sel, ew, out):
    es = ExitStack()
    with es:
        def sb(name, shape, dt=F32):
            return es.enter_context(nc.sbuf_tensor(name, shape, dt))

        def sem(name):
            return es.enter_context(nc.semaphore(name))

        bank = [es.enter_context(nc.psum_tensor(f"bank{i}", [128, 512], F32)) for i in range(8)]

        x_all = sb("x_all", [128, B * D])
        cT = sb("cT", [128, B * S])
        a = sb("a", [128, A_COLS])
        bo = sb("bo", [1, D])
        ones_row = sb("ones_row", [1, S])
        ones_sq = sb("ones_sq", [128, 128])
        maskb = sb("maskb", [128, 128], BF16)
        identb = sb("identb", [128, 128], BF16)
        fws = sb("fws", [128, 3 * INNER])
        lws = sb("lws", [128, L_COLS])
        sels = sb("sels", [3 * NR, NC * 128], BF16)
        ews = sb("ews", [128, NC * 3 * 128 + NR])
        tg = sb("tg", [128, 4])
        stats = sb("stats", [128, B * 6])
        mv = sb("mv", [128, B * 2])
        ve = sb("ve", [128, B])
        mhalf = sb("mhalf", [128, B])
        rstd = sb("rstd", [128, B])
        ident = a[:, A_ID:A_ID + 128]

        values = sb("values", [128, B * D])
        vm = sb("vm", [128, VH + VH + 128])
        W = HALF * 128
        xn = sb("xn", [128, 2, W])
        xnT = sb("xnT", [128, 2, W])
        full = sb("full", [128, 4, W])
        rest1 = sb("rest1", [128, 4, W])
        parts = sb("parts", [128, 4, 3, W], BF16)
        qx = sb("qx", [128, NG, B * S], BF16)
        kx = sb("kx", [128, NG, NJ, B * S], BF16)
        mx = sb("mx", [128, NB, 4])
        sx = sb("sx", [128, NB, W])
        pr = sb("pr", [128, NB, W])
        pT = sb("pT", [128, 2, W])
        gbo = sb("gbo", [128, D])
        rl = sb("rl", [128, S])
        oT = sb("oT", [128, S])

        fabs = sb("fabs", [128, 3])
        fmean = sb("fmean", [128, 3])
        fclip = sb("fclip", [128, 3])
        fscale = sb("fscale", [128, 3])
        fdeq = sb("fdeq", [128, 3])
        fq32 = sb("fq32", [128, 3 * INNER])
        fq = sb("fq", [128, 3, INNER], BF16)
        kxf = kx[:, :, :, :].rearrange("p g j t -> p (g j t)").bitcast(F32)
        f_xn = kxf[:, 0:B * D]
        f_t = kxf[:, B * D:2 * B * D]
        f_xq = sb("f_xq", [128, B * D], BF16)
        f_a = sb("f_a", [128, 4, B])
        f_deq = sb("f_deq", [128, 2, B])
        f_xqT = sb("f_xqT", [128, B * S], BF16)
        f_sil = kxf[:, 2 * B * D:3 * B * D].rearrange("p (u n) -> p u n", u=2)
        f_h = kxf[:, 3 * B * D:4 * B * D].rearrange("p (u n) -> p u n", u=2)
        f_ah = sb("f_ah", [128, 2, 5])
        f_ht = kxf[:, 4 * B * D:5 * B * D].rearrange("p (u n) -> p u n", u=2)
        f_hq = sb("f_hq", [128, 2, INNER], BF16)
        f_hqT = sb("f_hqT", [128, 2, INNER], BF16)

        kb = sb("kb", [128, 2, W])
        vb = sb("vb", [128, 2, W])
        n3, nT3 = full[:, 0:2, :], full[:, 2:4, :]
        q3, s3 = rest1[:, 0:2, :], rest1[:, 2:4, :]
        p3, pT3 = sx[:, 0:2, :], sx[:, 2:4, :]
        o3, oT3 = pr[:, 0:2, :], pr[:, 2:4, :]
        m3 = sb("m3", [128, 2, HALF * H])
        l3 = sb("l3", [128, 2, HALF * H])
        n4 = sb("n4", [128, 2, W])
        nT4 = sb("nT4", [128, 2, W])
        lg = sb("lg", [128, B, NR])
        top8 = sb("top8", [128, B, 8])
        top2 = sb("top2", [128, B, 8])
        rest = sb("rest", [128, B, NE])
        chosen = sb("chosen", [128, B, NE])
        le = sb("le", [128, B, NR])
        ex = sb("ex", [128, B, NR])
        exc = sb("exc", [128, B, NR])
        den = sb("den", [128, B, 2])
        rden = sb("rden", [128, B, 2])
        wt = sb("wt", [128, B, NR])
        whi = sb("whi", [128, B, 3, NR], BF16)
        wr1 = sb("wr1", [128, B, NR])
        wr2 = sb("wr2", [128, B, NR])
        wT = sb("wT", [3 * NR, B * S], BF16)
        e_sil = full[:, 0:2, :]
        e_t = full[:, 2:4, :]
        e_h = rest1[:, 0:2, :]

        names = """ld_x ld_c ld_a ld_r ld_f ld_l ld_s ld_e stored ident_ok const_ok gates_ok v_proj v_ok
            ln_stats ln_mv ln_ve ln_rstd
            a_xn a_xT a_xTs p_proj p_full p_hi p_r1 p_mid p_lo kx_zero kx_zero1 packed_q0 packed_q1 packed_k0 packed_k1
            gbo_ok x_bo vm_zero vm_ok a_vm a_S a_mx a_sub a_exp a_T a_Ts a_PV a_rl a_on a_y a_res
            w_abs w_sum w_mean w_clip w_scale w_deq w_r32 w_clipd w_q
            f_xstep f_deqr f_xqr f_xqTp f_xqTs f_gp f_up f_silr f_hr f_hstep f_htr f_hqr f_hTp f_hTs f_yp f_res
            k3p k3s v3p v3s n3r t3p t3s q3p q3s s3p m3r s3r p3r l3r r3r pt3p pt3s o3p o3r ot3p ot3s y3p x3r
            n4r t4p t4s lgp lgs r_top r_two r_rest r_chosen r_le r_ex r_exc r_den r_rden r_wt r_split wTp wTs
            e_Gp e_gp e_up e_silr e_tr e_hr e_yp e_res""".split()
        sm = {n: sem(n) for n in names}
        block = es.enter_context(nc.Block())

        def diagonal(u, half):
            at = u * VH + 64 * half
            return vm[:, at:at + 8 * DIAG].rearrange("p (h e) -> p h e", e=DIAG)[:, :, 0:DK]

        def tok(t, n, w=128):
            return t[:, bass.ts(n, w)]

        STEPS2 = 5

        @block.sync
        def _(sp):
            sp.dma_start(a[:, :], aw).then_inc(sm["ld_a"], 16)
            sp.dma_start(x_all[:, :], x).then_inc(sm["ld_x"], 16)
            sp.dma_start(fws[:, :], fw).then_inc(sm["ld_f"], 16)
            for s in range(2):
                sp.wait_ge(sm["p_lo"], 2 * s + 1)
                sp.wait_ge(sm["kx_zero1" if s else "kx_zero"], 1)
                for r in range(8):
                    for j in range(NJ):
                        sp.dma_start(kx[16 * r + 8 * j:16 * r + 8 * j + 8, :, j, s * W:(s + 1) * W],
                                     parts[64 * j:64 * j + 64, 2 * s, K_PART[r], :]).then_inc(sm[f"packed_k{s}"], 16)
                sp.wait_ge(sm["p_lo"], 2 * s + 2)
                for r in range(8):
                    sp.dma_start(qx[16 * r:16 * r + 16, :, s * W:(s + 1) * W],
                                 parts[:, 2 * s + 1, Q_PART[r], :]).then_inc(sm[f"packed_q{s}"], 16)
            sp.dma_start(ews[:, :], ew).then_inc(sm["ld_e"], 16)
            for s in range(2):
                sp.wait_ge(sm["e_res"], s + 1)
                sp.dma_start(out[:, s * W:(s + 1) * W], x_all[:, s * W:(s + 1) * W]).then_inc(sm["stored"], 16)
            sp.wait_ge(sm["stored"], 32)

        @block.gpsimd
        def _(pool):
            nc.gpsimd.memset(identb[:, :], 0.0).then_inc(sm["ident_ok"], 1)
            nc.gpsimd.memset(maskb[:, :], 0.0).then_inc(sm["ident_ok"], 1)
            pool.wait_ge(sm["ident_ok"], 2)
            nc.gpsimd.affine_select(out=identb[:, :], in_=identb[:, :], compare_op=ALU.not_equal, fill=1.0,
                                    base=0, pattern=[[-1, 128]], channel_multiplier=1).then_inc(sm["ident_ok"], 1)
            nc.gpsimd.affine_select(out=maskb[:, :], in_=maskb[:, :], compare_op=ALU.is_ge, fill=MASKED,
                                    base=0, pattern=[[-1, 128]], channel_multiplier=1).then_inc(sm["ident_ok"], 1)
            nc.gpsimd.memset(ones_row[:, :], 1.0).then_inc(sm["const_ok"], 1)
            nc.gpsimd.memset(ones_sq[:, :], 1.0).then_inc(sm["const_ok"], 1)
            nc.gpsimd.memset(mhalf[:, :], -0.5).then_inc(sm["const_ok"], 1)
            nc.gpsimd.memset(top2[:, :, :], 3e38).then_inc(sm["const_ok"], 1)
            pool.wait_ge(sm["const_ok"], 4)

            def rstd_of(r):
                pool.wait_ge(sm["ln_mv"], 8 * (r + 1))
                nc.gpsimd.tensor_scalar(ve[:, :], mv[:, :].rearrange("p (b t) -> p b t", t=2)[:, :, 1], EPS, None,
                                        ALU.add).then_inc(sm["ln_ve"], 1)
                pool.wait_ge(sm["ln_ve"], r + 1)
                nc.gpsimd.tensor_tensor(rstd[:, :], ve[:, :], mhalf[:, :], ALU.pow).then_inc(sm["ln_rstd"], 1)

            nc.gpsimd.memset(vm[:, :], 0.0).then_inc(sm["vm_zero"], 1)
            rstd_of(0)
            pool.wait_ge(sm["vm_zero"], 1)
            for u in range(2):
                nc.gpsimd.memset(diagonal(u, 1 - u), 1.0).then_inc(sm["vm_ok"], 1)
            nc.gpsimd.memset(kx[:, :, :, W:2 * W].bitcast(F32), 0.0).then_inc(sm["kx_zero1"], 1)
            pool.wait_ge(sm["gbo_ok"], 1)
            pool.wait_ge(sm["a_xn"], 2)
            nc.gpsimd.tensor_tensor(x_all[:, :].rearrange("p (b d) -> p b d", d=D),
                                    x_all[:, :].rearrange("p (b d) -> p b d", d=D),
                                    gbo[:, :].unsqueeze(1).to_broadcast([128, B, D]), ALU.add).then_inc(sm["x_bo"], 1)
            pool.wait_ge(sm["w_scale"], 1)
            for m in range(3):
                nc.gpsimd.tensor_scalar(fq32[:, bass.ts(m, INNER)], fws[:, bass.ts(m, INNER)], fscale[:, m:m + 1],
                                        MAGIC, ALU.mult, ALU.add).then_inc(sm["w_r32"], 1)
            for m in range(3):
                pool.wait_ge(sm["w_r32"], m + 1)
                nc.gpsimd.tensor_scalar(fq32[:, bass.ts(m, INNER)], fq32[:, bass.ts(m, INNER)], MAGIC, 1.0,
                                        ALU.subtract, ALU.min).then_inc(sm["w_clipd"], 1)
            for m in range(3):
                pool.wait_ge(sm["w_clipd"], m + 1)
                nc.gpsimd.tensor_scalar(fq[:, m, :], fq32[:, bass.ts(m, INNER)], -1.0, None,
                                        ALU.max).then_inc(sm["w_q"], 1)
            rstd_of(1)

            rstd_of(2)
            rstd_of(3)

        @block.scalar
        def _(act):
            act.dma_start(cT[:, 0:W], ctxT[:, 0:W]).then_inc(sm["ld_c"], 16)
            act.dma_start(cT[:, W:2 * W], ctxT[:, W:2 * W]).then_inc(sm["ld_c"], 16)
            act.dma_start(bo[:, :], rows).then_inc(sm["ld_r"], 16)
            act.dma_start(lws[:, :], lw).then_inc(sm["ld_l"], 16)
            act.dma_start(sels[:, :], sel).then_inc(sm["ld_s"], 16)
            act.wait_ge(sm["ld_a"], 16)
            nc.scalar.activation(tg[:, :], a[:, A_GX:A_GX + 4], ACT.Tanh).then_inc(sm["gates_ok"], 1)

            act.wait_ge(sm["gates_ok"], 1)
            nc.scalar.activation(gbo[:, :], a[:, A_BO:A_BO + D], ACT.Copy, scale=tg[:, 0:1]).then_inc(sm["gbo_ok"], 1)

            def project_copy(m):
                bias = a[:, A_BQ:A_BQ + 1] if m % 2 else a[:, A_BK:A_BK + 1]
                act.wait_ge(sm["p_proj"], m + 1)
                nc.scalar.activation(parts[:, m, 0, :], bank[m][:, :], ACT.Identity, bias=bias).then_inc(sm["p_hi"], 1)
                nc.scalar.activation(full[:, m, :], bank[m][:, :], ACT.Identity, bias=bias).then_inc(sm["p_full"], 1)

            def xT_copy(s):
                act.wait_ge(sm["a_xT"], s + 1)
                nc.scalar.activation(xnT[:, s, :], bank[6 + s][:, :], ACT.Copy).then_inc(sm["a_xTs"], 1)

            project_copy(0)
            xT_copy(0)
            project_copy(1)
            project_copy(2)
            xT_copy(1)
            project_copy(3)

            def attn(n, first):
                def exp(j):
                    act.wait_ge(sm["a_sub"], 4 * n + j + 1)
                    if not first:
                        act.wait_ge(sm["a_T"], 4 * n + j - 3)
                    nc.scalar.activation(pr[:, j, :], sx[:, j, :], ACT.Exp, scale=SCALE).then_inc(sm["a_exp"], 1)

                def pT_copy(j):
                    act.wait_ge(sm["a_T"], 4 * n + j + 1)
                    if not first or j >= 2:
                        act.wait_ge(sm["a_PV"], 4 * n + j - 1)
                    nc.scalar.activation(pT[:, j % 2, :], bank[4 + j % 2][:, :], ACT.Copy).then_inc(sm["a_Ts"], 1)

                def masked_values(u):
                    if not first:
                        act.wait_ge(sm["a_PV"], 4 * n - 2 + 2 * u)
                    nc.scalar.activation(diagonal(u, u), values[:, bass.ds(n * D + 64 * u, 64)]
                                         .rearrange("p (h e) -> p h e", e=DK), ACT.Copy).then_inc(sm["a_vm"], 1)

                exp(0)
                masked_values(0)
                exp(1)
                pT_copy(0)
                exp(2)
                masked_values(1)
                pT_copy(1)
                exp(3)
                pT_copy(2)
                pT_copy(3)

            act.wait_ge(sm["v_ok"], 2)
            act.wait_ge(sm["vm_ok"], 2)
            attn(0, True)
            with act.Fori(1, B) as n:
                attn(n, False)

            act.wait_ge(sm["f_xqTp"], 1)
            nc.scalar.activation(f_xqT[:, :], bank[0][:, :].bitcast(BF16), ACT.Copy).then_inc(sm["f_xqTs"], 1)

            act.wait_ge(sm["f_deqr"], 2)

            def silu(n, u):
                act.wait_ge(sm["f_gp"], n + 1)
                nc.scalar.activation(f_sil[:, u, :], bank[1 + u][:, :], ACT.Silu,
                                     scale=f_deq[:, 0, bass.ds(n, 1)]).then_inc(sm["f_silr"], 1)

            def hidden_scale(n, u):
                act.wait_ge(sm["f_hstep"], STEPS2 * n + 4)
                nc.scalar.activation(f_ht[:, u, :], f_h[:, u, :], ACT.Identity,
                                     scale=f_ah[:, u, 2:3]).then_inc(sm["f_htr"], 1)

            def hT_copy(n, u):
                act.wait_ge(sm["f_hTp"], n + 1)
                nc.scalar.activation(f_hqT[:, u, :], bank[5][:, :].bitcast(BF16)[:, 0:INNER],
                                     ACT.Copy).then_inc(sm["f_hTs"], 1)

            def ffn(n, u, last):
                if not last:
                    silu(n + 1, 1 - u)
                hidden_scale(n, u)
                hT_copy(n, u)

            silu(0, 0)
            with act.Fori(0, B // 2 - 1) as i:
                ffn(2 * i, 0, False)
                ffn(2 * i + 1, 1, False)
            ffn(B - 2, 0, False)
            ffn(B - 1, 1, True)

            for s in range(2):
                act.wait_ge(sm["t3p"], s + 1)
                nc.scalar.activation(nT3[:, s, :], bank[s][:, :], ACT.Copy).then_inc(sm["t3s"], 1)
            for s in range(2):
                act.wait_ge(sm["q3p"], s + 1)
                nc.scalar.activation(q3[:, s, :], bank[s][:, :], ACT.Identity,
                                     bias=lws[:, L_BQ:L_BQ + 1]).then_inc(sm["q3s"], 1)
            for s in range(2):
                act.wait_ge(sm["s3r"], s + 1)
                nc.scalar.activation(p3[:, s, :], s3[:, s, :], ACT.Exp, scale=SCALE).then_inc(sm["p3r"], 1)
            for s in range(2):
                act.wait_ge(sm["pt3p"], s + 1)
                nc.scalar.activation(pT3[:, s, :], bank[s][:, :], ACT.Copy).then_inc(sm["pt3s"], 1)
            for s in range(2):
                act.wait_ge(sm["ot3p"], s + 1)
                nc.scalar.activation(oT3[:, s, :], bank[s][:, :], ACT.Identity,
                                     bias=lws[:, L_BV:L_BV + 1]).then_inc(sm["ot3s"], 1)

            for s in range(2):
                act.wait_ge(sm["t4p"], s + 1)
                nc.scalar.activation(nT4[:, s, :], bank[s][:, :], ACT.Copy).then_inc(sm["t4s"], 1)
            act.wait_ge(sm["lgp"], 1)
            nc.scalar.activation(lg[:, :, :], bank[4][:, 0:B * NR].rearrange("p (b e) -> p b e", e=NR),
                                 ACT.Copy).then_inc(sm["lgs"], 1)
            act.wait_ge(sm["r_le"], 2)
            nc.scalar.activation(ex[:, :, :], le[:, :, :], ACT.Exp).then_inc(sm["r_ex"], 1)
            for s in range(2):
                act.wait_ge(sm["wTp"], s + 1)
                nc.scalar.activation(wT[:, s * W:(s + 1) * W], bank[5 + s][:, :].bitcast(BF16)[0:3 * NR, 0:W],
                                     ACT.Copy).then_inc(sm["wTs"], 1)

            for k in range(2 * NC):
                act.wait_ge(sm["e_gp"], k + 1)
                if k >= 2:
                    act.wait_ge(sm["e_tr"], k - 1)
                nc.scalar.activation(e_sil[:, k % 2, :], bank[k % 2][:, :], ACT.Silu).then_inc(sm["e_silr"], 1)

        @block.vector
        def _(dve):
            V = nc.vector

            def aggregate(r):
                dve.wait_ge(sm["ln_stats"], B * (r + 1))
                for b in range(B):
                    V.bn_aggr(mv[:, 2 * b:2 * b + 2], stats[:, 6 * b:6 * b + 6]).then_inc(sm["ln_mv"], 1)
                dve.wait_ge(sm["ln_mv"], B * (r + 1))
                dve.wait_ge(sm["ln_rstd"], r + 1)

            def normalize(dst, n):
                return V.tensor_scalar(dst, tok(x_all, n), mv[:, bass.ds(2 * n, 1)], rstd[:, bass.ds(n, 1)],
                                       ALU.subtract, ALU.mult)

            V.memset(kx[:, :, :, 0:W].bitcast(F32), 0.0).then_inc(sm["kx_zero"], 1)
            dve.wait_ge(sm["ld_x"], 16)
            for b in range(B):
                V.bn_stats(stats[:, 6 * b:6 * b + 6], x_all[:, b * D:(b + 1) * D]).then_inc(sm["ln_stats"], 1)
            aggregate(0)
            for s in range(2):
                for b in range(HALF):
                    last = normalize(xn[:, s, b * D:(b + 1) * D], HALF * s + b)
                last.then_inc(sm["a_xn"], 1)

            def split(m):
                dve.wait_ge(sm["p_full"], m + 1)
                V.tensor_tensor(rest1[:, m, :], full[:, m, :], parts[:, m, 0, :], ALU.subtract).then_inc(sm["p_r1"], 1)
                dve.wait_ge(sm["p_r1"], m + 1)
                V.tensor_copy(parts[:, m, 1, :], rest1[:, m, :]).then_inc(sm["p_mid"], 1)
                dve.wait_ge(sm["p_mid"], m + 1)
                V.tensor_tensor(parts[:, m, 2, :], rest1[:, m, :], parts[:, m, 1, :],
                                ALU.subtract).then_inc(sm["p_lo"], 1)

            split(0)
            split(1)
            for s in range(2):
                dve.wait_ge(sm["v_proj"], s + 1)
                V.tensor_tensor(values[:, s * W:(s + 1) * W].rearrange("p (b d) -> p b d", d=D),
                                bank[4 + s][:, :].rearrange("p (b d) -> p b d", d=D),
                                a[:, A_BV:A_BV + D].unsqueeze(1).to_broadcast([128, HALF, D]),
                                ALU.add).then_inc(sm["v_ok"], 1)
            split(2)
            split(3)
            dve.wait_ge(sm["ld_f"], 16)
            V.tensor_reduce(fabs[:, :], fws[:, :].rearrange("p (m n) -> p m n", m=3), AX.X, ALU.add,
                            apply_absolute_value=True).then_inc(sm["w_abs"], 1)
            dve.wait_ge(sm["w_sum"], 1)
            V.tensor_scalar(fmean[:, :], bank[0][:, 0:3], 1.0 / (INNER * D), None, ALU.mult).then_inc(sm["w_mean"], 1)
            dve.wait_ge(sm["w_mean"], 1)
            V.tensor_scalar(fclip[:, :], fmean[:, :], QMIN, None, ALU.max).then_inc(sm["w_clip"], 1)
            dve.wait_ge(sm["w_clip"], 1)
            V.reciprocal(fscale[:, :], fclip[:, :]).then_inc(sm["w_scale"], 1)
            V.tensor_scalar(fdeq[:, 0:2], fclip[:, 0:2], 1.0 / 127.0, None, ALU.mult).then_inc(sm["w_deq"], 1)
            V.tensor_scalar(fdeq[:, 2:3], fclip[:, 2:3], 1.0 / 127.0, tg[:, 2:3], ALU.mult, ALU.mult)\
                .then_inc(sm["w_deq"], 1)
            dve.wait_ge(sm["ld_l"], 16)
            for s in range(2):
                dve.wait_ge(sm["k3p"], s + 1)
                V.scalar_tensor_tensor(kb[:, s, :].rearrange("p (b t) -> p b t", b=HALF),
                                       bank[6 + s][:, :].rearrange("p (b t) -> p b t", b=HALF), lws[:, L_BK:L_BK + 1],
                                       lws[:, L_MK:L_MK + S].unsqueeze(1).to_broadcast([128, HALF, S]),
                                       ALU.add, ALU.mult).then_inc(sm["k3s"], 1)
                dve.wait_ge(sm["v3p"], s + 1)
                V.tensor_tensor(vb[:, s, :].rearrange("p (b t) -> p b t", b=HALF),
                                bank[4 + s][:, :].rearrange("p (b t) -> p b t", b=HALF),
                                lws[:, L_MV:L_MV + D].unsqueeze(1).to_broadcast([128, HALF, D]),
                                ALU.mult).then_inc(sm["v3s"], 1)

            def heads_out(n, u):
                dve.wait_ge(sm["a_PV"], 4 * n + 2 * u + 2)
                V.reciprocal(rl[64 * u:64 * u + 64, :],
                             bank[6 + u][64 - 64 * u:128 - 64 * u, 0:S]).then_inc(sm["a_rl"], 1)
                dve.wait_ge(sm["a_rl"], 2 * n + u + 1)
                V.tensor_tensor(oT[64 * u:64 * u + 64, :], bank[6 + u][64 * u:64 * u + 64, 0:S],
                                rl[64 * u:64 * u + 64, :], ALU.mult).then_inc(sm["a_on"], 1)

            def residual(n):
                dve.wait_ge(sm["a_y"], n + 1)
                V.scalar_tensor_tensor(tok(x_all, n), bank[7][:, S:2 * S], tg[:, 0:1], tok(x_all, n),
                                       ALU.mult, ALU.add).then_inc(sm["a_res"], 1)
                dve.wait_ge(sm["a_res"], n + 1)
                V.bn_stats(tok(stats, n, 6), tok(x_all, n)).then_inc(sm["ln_stats"], 1)

            def attn(n, before, before2):
                def top(j):
                    dve.wait_ge(sm["a_S"], 4 * n + j + 1)
                    V.tensor_reduce(mx[:, j, :], bank[j][:, :].rearrange("p (h k) -> p h k", h=4), AX.X,
                                    ALU.max).then_inc(sm["a_mx"], 1)

                def sub(j):
                    dve.wait_ge(sm["a_mx"], 4 * n + j + 1)
                    if before:
                        dve.wait_ge(sm["a_exp"], 4 * n + j - 3)
                    V.tensor_tensor(sx[:, j, :].rearrange("p (h k) -> p h k", h=4),
                                    bank[j][:, :].rearrange("p (h k) -> p h k", h=4),
                                    mx[:, j, :].unsqueeze(2).to_broadcast([128, 4, S]),
                                    ALU.subtract).then_inc(sm["a_sub"], 1)

                top(0)
                sub(0)
                if before2:
                    residual(n - 2)
                top(1)
                sub(1)
                if before:
                    heads_out(n - 1, 0)
                top(2)
                sub(2)
                top(3)
                sub(3)
                if before:
                    heads_out(n - 1, 1)

            dve.wait_ge(sm["x_bo"], 1)
            attn(0, False, False)
            attn(1, True, False)
            with dve.Fori(2, B) as n:
                attn(n, True, True)
            residual(B - 2)
            heads_out(B - 1, 0)
            heads_out(B - 1, 1)
            residual(B - 1)

            aggregate(1)

            xn_b = f_xn.rearrange("p (b d) -> p b d", d=D)
            for b in range(B):
                last = normalize(f_xn[:, b * D:(b + 1) * D], b)
            last.then_inc(sm["f_xstep"], 1)
            dve.wait_ge(sm["f_xstep"], 1)
            V.tensor_reduce(f_a[:, 0, :], xn_b, AX.X, ALU.max, apply_absolute_value=True).then_inc(sm["f_xstep"], 1)
            dve.wait_ge(sm["f_xstep"], 2)
            V.tensor_scalar(f_a[:, 1, :], f_a[:, 0, :], QMIN, None, ALU.max).then_inc(sm["f_xstep"], 1)
            dve.wait_ge(sm["f_xstep"], 3)
            V.reciprocal(f_a[:, 2, :], f_a[:, 1, :]).then_inc(sm["f_xstep"], 1)
            dve.wait_ge(sm["f_xstep"], 4)
            V.tensor_scalar(f_a[:, 3, :], f_a[:, 2, :], 127.0, None, ALU.mult).then_inc(sm["f_xstep"], 1)
            dve.wait_ge(sm["w_deq"], 2)
            V.tensor_scalar(f_deq[:, 0, :], f_a[:, 1, :], fdeq[:, 0:1], None, ALU.mult).then_inc(sm["f_deqr"], 1)
            V.tensor_scalar(f_deq[:, 1, :], f_a[:, 1, :], fdeq[:, 1:2], None, ALU.mult).then_inc(sm["f_deqr"], 1)
            dve.wait_ge(sm["f_xstep"], 5)
            V.tensor_tensor(f_t.rearrange("p (b d) -> p b d", d=D), xn_b,
                            f_a[:, 3, :].unsqueeze(2).to_broadcast([128, B, D]), ALU.mult).then_inc(sm["f_xstep"], 1)
            dve.wait_ge(sm["f_xstep"], 6)
            V.tensor_scalar(f_xq[:, :], f_t, MAGIC, MAGIC, ALU.add, ALU.subtract).then_inc(sm["f_xqr"], 1)

            def hidden_round(n, u):
                dve.wait_ge(sm["f_htr"], n + 1)
                V.tensor_scalar(f_hq[:, u, :], f_ht[:, u, :], MAGIC, MAGIC,
                                ALU.add, ALU.subtract).then_inc(sm["f_hqr"], 1)

            def ffn_residual(n, u):
                dve.wait_ge(sm["f_yp"], n + 1)
                V.scalar_tensor_tensor(tok(x_all, n), bank[6][:, 0:D], f_ah[:, u, 3:4], tok(x_all, n),
                                       ALU.mult, ALU.add).then_inc(sm["f_res"], 1)

            def ffn_stats(n):
                dve.wait_ge(sm["f_res"], n + 1)
                V.bn_stats(tok(stats, n, 6), tok(x_all, n)).then_inc(sm["ln_stats"], 1)

            def ffn(n, u, first):
                at = lambda k: STEPS2 * n + k
                dve.wait_ge(sm["f_up"], n + 1)
                dve.wait_ge(sm["f_silr"], n + 1)
                V.scalar_tensor_tensor(f_h[:, u, :], bank[3 + u][:, :], f_deq[:, 1, bass.ds(n, 1)], f_sil[:, u, :],
                                       ALU.mult, ALU.mult).then_inc(sm["f_hr"], 1)
                if not first:
                    hidden_round(n - 1, 1 - u)
                dve.wait_ge(sm["f_hr"], n + 1)
                V.tensor_reduce(f_ah[:, u, 0:1], f_h[:, u, :], AX.X, ALU.max,
                                apply_absolute_value=True).then_inc(sm["f_hstep"], 1)
                dve.wait_ge(sm["f_hstep"], at(1))
                V.tensor_scalar(f_ah[:, u, 1:2], f_ah[:, u, 0:1], QMIN, None, ALU.max).then_inc(sm["f_hstep"], 1)
                dve.wait_ge(sm["f_hstep"], at(2))
                V.reciprocal(f_ah[:, u, 4:5], f_ah[:, u, 1:2]).then_inc(sm["f_hstep"], 1)
                dve.wait_ge(sm["f_hstep"], at(3))
                V.tensor_scalar(f_ah[:, u, 2:3], f_ah[:, u, 4:5], 127.0, None, ALU.mult).then_inc(sm["f_hstep"], 1)
                if not first:
                    ffn_residual(n - 1, 1 - u)
                V.tensor_scalar(f_ah[:, u, 3:4], f_ah[:, u, 1:2], fdeq[:, 2:3], None, ALU.mult).then_inc(sm["f_hstep"], 1)
                if not first:
                    ffn_stats(n - 1)

            ffn(0, 0, True)
            with dve.Fori(0, B // 2 - 1) as i:
                ffn(2 * i + 1, 1, False)
                ffn(2 * i + 2, 0, False)
            ffn(B - 1, 1, False)
            hidden_round(B - 1, 1)
            dve.wait_ge(sm["f_hstep"], STEPS2 * B)
            ffn_residual(B - 1, 1)
            ffn_stats(B - 1)

            aggregate(2)
            for s in range(2):
                for b in range(HALF):
                    last = normalize(n3[:, s, b * D:(b + 1) * D], HALF * s + b)
                last.then_inc(sm["n3r"], 1)
            for s in range(2):
                dve.wait_ge(sm["s3p"], s + 1)
                sc = bank[2 + s][:, :].rearrange("p (b j h) -> p b h j", b=HALF, h=H)
                V.tensor_reduce(m3[:, s, :].rearrange("p (b h) -> p b h", h=H), sc, AX.X, ALU.max).then_inc(sm["m3r"], 1)
            for s in range(2):
                dve.wait_ge(sm["m3r"], s + 1)
                V.tensor_tensor(s3[:, s, :].rearrange("p (b j h) -> p b j h", b=HALF, h=H),
                                bank[2 + s][:, :].rearrange("p (b j h) -> p b j h", b=HALF, h=H),
                                m3[:, s, :].rearrange("p (b h) -> p b h", h=H).unsqueeze(2)
                                .to_broadcast([128, HALF, KEYS, H]), ALU.subtract).then_inc(sm["s3r"], 1)
            for s in range(2):
                dve.wait_ge(sm["p3r"], s + 1)
                V.tensor_reduce(m3[:, s, :].rearrange("p (b h) -> p b h", h=H),
                                p3[:, s, :].rearrange("p (b j h) -> p b h j", b=HALF, h=H), AX.X,
                                ALU.add).then_inc(sm["l3r"], 1)
            for s in range(2):
                dve.wait_ge(sm["l3r"], s + 1)
                V.reciprocal(l3[:, s, :], m3[:, s, :]).then_inc(sm["r3r"], 1)
            for s in range(2):
                dve.wait_ge(sm["o3p"], s + 1)
                dve.wait_ge(sm["r3r"], s + 1)
                V.tensor_tensor(o3[:, s, :].rearrange("p (n e) -> p n e", e=DK),
                                bank[4 + s][:, :].rearrange("p (n e) -> p n e", e=DK),
                                l3[:, s, :].unsqueeze(2).to_broadcast([128, HALF * H, DK]),
                                ALU.mult).then_inc(sm["o3r"], 1)
            for s in range(2):
                dve.wait_ge(sm["y3p"], s + 1)
                xs = x_all[:, s * W:(s + 1) * W]
                V.scalar_tensor_tensor(xs, bank[6 + s][:, :], tg[:, 1:2], xs, ALU.mult, ALU.add).then_inc(sm["x3r"], 1)
            for b in range(B):
                dve.wait_ge(sm["x3r"], b // HALF + 1)
                V.bn_stats(stats[:, 6 * b:6 * b + 6], x_all[:, b * D:(b + 1) * D]).then_inc(sm["ln_stats"], 1)

            aggregate(3)
            for s in range(2):
                for b in range(HALF):
                    last = normalize(n4[:, s, b * D:(b + 1) * D], HALF * s + b)
                last.then_inc(sm["n4r"], 1)
            dve.wait_ge(sm["const_ok"], 4)
            dve.wait_ge(sm["lgs"], 1)
            for b in range(B):
                V.max(top8[:, b, :], lg[:, b, 0:NE]).then_inc(sm["r_top"], 1)
            dve.wait_ge(sm["r_top"], B)
            V.tensor_copy(top2[:, :, 0:2], top8[:, :, 0:2]).then_inc(sm["r_two"], 1)
            V.tensor_tensor(le[:, :, 0:NE], lg[:, :, 0:NE], top8[:, :, 0:1].to_broadcast([128, B, NE]),
                            ALU.subtract).then_inc(sm["r_le"], 1)
            V.tensor_scalar(le[:, :, NE:NR], lg[:, :, NE:NR], -1.0, None, ALU.mult).then_inc(sm["r_le"], 1)
            dve.wait_ge(sm["r_two"], 1)
            for b in range(B):
                V.match_replace(rest[:, b, :], top2[:, b, :], lg[:, b, 0:NE], MASKED).then_inc(sm["r_rest"], 1)
            dve.wait_ge(sm["r_rest"], B)
            V.tensor_tensor(chosen[:, :, :], rest[:, :, :], lg[:, :, 0:NE], ALU.not_equal).then_inc(sm["r_chosen"], 1)
            dve.wait_ge(sm["r_chosen"], 1)
            dve.wait_ge(sm["r_ex"], 1)
            V.tensor_tensor(exc[:, :, 0:NE], ex[:, :, 0:NE], chosen[:, :, :], ALU.mult).then_inc(sm["r_exc"], 1)
            V.tensor_scalar(den[:, :, 1:2], ex[:, :, NE:NR], 1.0, None, ALU.add).then_inc(sm["r_den"], 1)
            V.memset(exc[:, :, NE:NR], 1.0).then_inc(sm["r_exc"], 1)
            dve.wait_ge(sm["r_exc"], 2)
            V.tensor_reduce(den[:, :, 0:1], exc[:, :, 0:NE], AX.X, ALU.add).then_inc(sm["r_den"], 1)
            dve.wait_ge(sm["r_den"], 2)
            V.reciprocal(rden[:, :, :], den[:, :, :]).then_inc(sm["r_rden"], 1)
            dve.wait_ge(sm["r_rden"], 1)
            V.tensor_tensor(wt[:, :, 0:NE], exc[:, :, 0:NE], rden[:, :, 0:1].to_broadcast([128, B, NE]),
                            ALU.mult).then_inc(sm["r_wt"], 1)
            V.tensor_tensor(wt[:, :, NE:NR], exc[:, :, NE:NR], rden[:, :, 1:2], ALU.mult).then_inc(sm["r_wt"], 1)
            dve.wait_ge(sm["r_wt"], 2)
            V.tensor_copy(whi[:, :, 0, :], wt[:, :, :]).then_inc(sm["r_split"], 1)
            dve.wait_ge(sm["r_split"], 1)
            V.tensor_tensor(wr1[:, :, :], wt[:, :, :], whi[:, :, 0, :], ALU.subtract).then_inc(sm["r_split"], 1)
            dve.wait_ge(sm["r_split"], 2)
            V.tensor_copy(whi[:, :, 1, :], wr1[:, :, :]).then_inc(sm["r_split"], 1)
            dve.wait_ge(sm["r_split"], 3)
            V.tensor_tensor(whi[:, :, 2, :], wr1[:, :, :], whi[:, :, 1, :], ALU.subtract).then_inc(sm["r_split"], 1)

            for k in range(2 * NC):
                s, c, u = k // NC, k % NC, k % 2
                dve.wait_ge(sm["e_silr"], k + 1)
                dve.wait_ge(sm["e_up"], k + 1)
                V.tensor_tensor(e_t[:, u, :], e_sil[:, u, :], bank[2 + u][:, :], ALU.mult).then_inc(sm["e_tr"], 1)
                dve.wait_ge(sm["e_tr"], k + 1)
                dve.wait_ge(sm["e_Gp"], k + 1)
                if k >= 2:
                    dve.wait_ge(sm["e_yp"], k - 1)
                V.tensor_tensor(e_h[:, u, :], e_t[:, u, :], bank[4 + u][:, :], ALU.mult).then_inc(sm["e_hr"], 1)
                if c == NC - 1:
                    dve.wait_ge(sm["e_yp"], k + 1)
                    xs = x_all[:, s * W:(s + 1) * W]
                    V.scalar_tensor_tensor(xs, bank[6 + s][:, :], tg[:, 3:4], xs, ALU.mult, ALU.add)\
                        .then_inc(sm["e_res"], 1)

        @block.tensor
        def _(pe):
            mm = nc.tensor.matmul
            pe.wait_ge(sm["ld_a"], 16)
            pe.wait_ge(sm["ld_c"], 32)
            pe.wait_ge(sm["const_ok"], 4)
            def q_proj(s):
                pe.wait_ge(sm["a_xn"], s + 1)
                for b in range(HALF):
                    last = nc.tensor.transpose(bank[6 + s][:, b * S:(b + 1) * S], xn[:, s, b * D:(b + 1) * D], ident)
                last.then_inc(sm["a_xT"], 1)
                pe.wait_ge(sm["a_xTs"], s + 1)
                mm(bank[2 * s + 1][:, :], a[:, A_WQ:A_WQ + D], xnT[:, s, :], start=True, stop=True)\
                    .then_inc(sm["p_proj"], 1)

            def k_proj(s):
                mm(bank[2 * s][:, :], a[:, A_WK:A_WK + D], cT[:, s * W:(s + 1) * W], start=True, stop=True)\
                    .then_inc(sm["p_proj"], 1)

            k_proj(0)
            q_proj(0)
            k_proj(1)
            q_proj(1)
            for s in range(2):
                for b in range(HALF):
                    last = mm(bank[4 + s][:, b * D:(b + 1) * D], cT[:, (HALF * s + b) * S:(HALF * s + b + 1) * S],
                              a[:, A_WV:A_WV + D], start=True, stop=True)
                last.then_inc(sm["v_proj"], 1)

            pe.wait_ge(sm["ld_l"], 16)
            for s in range(2):
                pe.wait_ge(sm["a_xTs"], s + 1)
                mm(bank[6 + s][:, :], lws[:, L_WK:L_WK + D], cT[:, s * W:(s + 1) * W],
                   start=True, stop=True).then_inc(sm["k3p"], 1)
                pe.wait_ge(sm["v_ok"], s + 1)
                for b in range(HALF):
                    n = HALF * s + b
                    last = mm(bank[4 + s][:, b * D:(b + 1) * D], cT[:, n * S:(n + 1) * S], lws[:, L_WV:L_WV + D],
                              start=True, stop=True)
                last.then_inc(sm["v3p"], 1)
            pe.wait_ge(sm["w_abs"], 1)
            pe.wait_ge(sm["p_full"], 1)
            mm(bank[0][:, 0:3], ones_sq[:, :], fabs[:, :], start=True, stop=True).then_inc(sm["w_sum"], 1)

            def y_proj(n):
                pe.wait_ge(sm["a_on"], 2 * n + 2)
                mm(bank[7][:, S:2 * S], oT[:, :], a[:, A_WO:A_WO + D], start=True, stop=True).then_inc(sm["a_y"], 1)

            def score(n, j, first):
                if not first:
                    pe.wait_ge(sm["a_sub"], 4 * n + j - 3)
                else:
                    pe.wait_ge(sm["p_full"], j + 1)
                mm(bank[j][:, :], identb[:, :], maskb[:, :].unsqueeze(1).to_broadcast([128, 4, S]),
                   start=True, stop=False)
                for t in range(2):
                    last = mm(bank[j][:, t * 2 * S:(t + 1) * 2 * S], qx[:, 2 * j + t, bass.ts(n, S)],
                              kx[:, 2 * j + t, :, bass.ts(n, S)], start=False, stop=(t == 1))
                last.then_inc(sm["a_S"], 1)

            def attn(n, first, last_one):
                def next_score(j):
                    if not last_one:
                        score(n + 1, j, False)

                def transposes(j):
                    pe.wait_ge(sm["a_exp"], 4 * n + j + 1)
                    if not first or j >= 2:
                        pe.wait_ge(sm["a_Ts"], 4 * n + j - 1)
                    for g in range(4):
                        last = nc.tensor.transpose(bank[4 + j % 2][:, g * S:(g + 1) * S],
                                                   pr[:, j, g * S:(g + 1) * S], ident)
                    last.then_inc(sm["a_T"], 1)

                def pv(j):
                    u = j // 2
                    pe.wait_ge(sm["a_Ts"], 4 * n + j + 1)
                    if j % 2 == 0:
                        pe.wait_ge(sm["a_vm"], 2 * n + u + 1)
                        if not first:
                            if u == 0:
                                pe.wait_ge(sm["a_on"], 2 * n - 1)
                            else:
                                pe.wait_ge(sm["a_res"], n)
                    for g in range(4):
                        h = 4 * j + g
                        last = mm(bank[6 + u][:, 0:S], vm[:, h * 128:(h + 1) * 128], pT[:, j % 2, g * S:(g + 1) * S],
                                  start=(h % 8 == 0), stop=(h % 8 == 7))
                    last.then_inc(sm["a_PV"], 1)

                transposes(0)
                next_score(0)
                transposes(1)
                pv(0)
                if not first:
                    y_proj(n - 1)
                next_score(1)
                transposes(2)
                pv(1)
                next_score(2)
                transposes(3)
                pv(2)
                next_score(3)
                pv(3)

            pe.wait_ge(sm["ident_ok"], 4)
            pe.wait_ge(sm["w_mean"], 1)
            pe.wait_ge(sm["k3s"], 2)
            pe.wait_ge(sm["v3s"], 2)
            pe.wait_ge(sm["packed_k0"], 16 * 16)
            pe.wait_ge(sm["packed_q0"], 16 * 8)
            for j in range(NB):
                score(0, j, True)
            attn(0, True, False)
            with pe.Fori(1, HALF - 1) as n:
                attn(n, False, False)
            pe.wait_ge(sm["packed_k1"], 16 * 16)
            pe.wait_ge(sm["packed_q1"], 16 * 8)
            with pe.Fori(HALF - 1, B - 1) as n:
                attn(n, False, False)
            attn(B - 1, False, True)
            y_proj(B - 1)

            pe.wait_ge(sm["f_xqr"], 1)
            for b in range(B):
                last = nc.tensor.transpose(bank[0][:, :].bitcast(BF16)[:, b * S:(b + 1) * S],
                                           f_xq[:, b * D:(b + 1) * D], identb[:, :])
            last.then_inc(sm["f_xqTp"], 1)
            pe.wait_ge(sm["f_xqTs"], 1)
            pe.wait_ge(sm["w_q"], 3)

            def gate_up(n, u, first):
                if not first:
                    pe.wait_ge(sm["f_silr"], n - 1)
                    pe.wait_ge(sm["f_hr"], n - 1)
                mm(bank[1 + u][:, :], f_xqT[:, bass.ts(n, S)], fq[:, 0, :], start=True, stop=True).then_inc(sm["f_gp"], 1)
                mm(bank[3 + u][:, :], f_xqT[:, bass.ts(n, S)], fq[:, 1, :], start=True, stop=True).then_inc(sm["f_up"], 1)

            def down(n, u, first):
                pe.wait_ge(sm["f_hqr"], n + 1)
                if not first:
                    pe.wait_ge(sm["f_hTs"], n)
                for c in range(4):
                    last = nc.tensor.transpose(bank[5][:, :].bitcast(BF16)[:, c * S:(c + 1) * S],
                                               f_hq[:, u, c * 128:(c + 1) * 128], identb[:, :])
                last.then_inc(sm["f_hTp"], 1)
                pe.wait_ge(sm["f_hTs"], n + 1)
                if not first:
                    pe.wait_ge(sm["f_res"], n)
                for c in range(4):
                    last = mm(bank[6][:, 0:D], f_hqT[:, u, c * S:(c + 1) * S], fq[:, 2, c * D:(c + 1) * D],
                              start=(c == 0), stop=(c == 3))
                last.then_inc(sm["f_yp"], 1)

            gate_up(0, 0, True)
            gate_up(1, 1, True)
            gate_up(2, 0, False)
            down(0, 0, True)
            with pe.Fori(0, (B - 4) // 2) as i:
                gate_up(2 * i + 3, 1, False)
                down(2 * i + 1, 1, False)
                gate_up(2 * i + 4, 0, False)
                down(2 * i + 2, 0, False)
            gate_up(B - 1, 1, False)
            down(B - 3, 1, False)
            down(B - 2, 0, False)
            down(B - 1, 1, False)

            hb = lambda s, b: slice((HALF * s + b) * S, (HALF * s + b + 1) * S)
            pe.wait_ge(sm["k3s"], 2)
            pe.wait_ge(sm["v3s"], 2)
            pe.wait_ge(sm["ld_r"], 16)
            pe.wait_ge(sm["f_res"], B)
            for s in range(2):
                pe.wait_ge(sm["n3r"], s + 1)
                for b in range(HALF):
                    last = nc.tensor.transpose(bank[s][:, b * S:(b + 1) * S], n3[:, s, b * D:(b + 1) * D], ident)
                last.then_inc(sm["t3p"], 1)
            for s in range(2):
                pe.wait_ge(sm["t3s"], s + 1)
                mm(bank[s][:, :], lws[:, L_WQ:L_WQ + D], nT3[:, s, :], start=True, stop=True).then_inc(sm["q3p"], 1)
            for s in range(2):
                pe.wait_ge(sm["q3s"], s + 1)
                for b in range(HALF):
                    last = mm(bank[2 + s][:, b * S:(b + 1) * S], q3[:, s, b * S:(b + 1) * S],
                              kb[:, s, b * S:(b + 1) * S], start=True, stop=True)
                last.then_inc(sm["s3p"], 1)
            for s in range(2):
                pe.wait_ge(sm["p3r"], s + 1)
                for b in range(HALF):
                    last = nc.tensor.transpose(bank[s][:, b * S:(b + 1) * S], p3[:, s, b * S:(b + 1) * S], ident)
                last.then_inc(sm["pt3p"], 1)
            for s in range(2):
                pe.wait_ge(sm["pt3s"], s + 1)
                for b in range(HALF):
                    last = mm(bank[4 + s][:, b * S:(b + 1) * S], pT3[:, s, b * S:(b + 1) * S],
                              vb[:, s, b * S:(b + 1) * S], start=True, stop=True)
                last.then_inc(sm["o3p"], 1)
            for s in range(2):
                pe.wait_ge(sm["o3r"], s + 1)
                for b in range(HALF):
                    last = nc.tensor.transpose(bank[s][:, b * S:(b + 1) * S], o3[:, s, b * D:(b + 1) * D], ident)
                last.then_inc(sm["ot3p"], 1)
            for s in range(2):
                pe.wait_ge(sm["ot3s"], s + 1)
                mm(bank[6 + s][:, :], ones_row[:, :], bo[:, :].unsqueeze(1).to_broadcast([1, HALF, D]),
                   start=True, stop=False)
                for b in range(HALF):
                    last = mm(bank[6 + s][:, b * D:(b + 1) * D], oT3[:, s, b * S:(b + 1) * S], lws[:, L_WO:L_WO + D],
                              start=False, stop=(b == HALF - 1))
                last.then_inc(sm["y3p"], 1)

            for s in range(2):
                pe.wait_ge(sm["n4r"], s + 1)
                for b in range(HALF):
                    last = nc.tensor.transpose(bank[s][:, b * S:(b + 1) * S], n4[:, s, b * D:(b + 1) * D], ident)
                last.then_inc(sm["t4p"], 1)
            for s in range(2):
                pe.wait_ge(sm["ld_e"], 16)
                pe.wait_ge(sm["t4s"], s + 1)
                for b in range(HALF):
                    n = HALF * s + b
                    last = mm(bank[4][:, n * NR:(n + 1) * NR], nT4[:, s, b * S:(b + 1) * S],
                              ews[:, NC * 3 * 128:NC * 3 * 128 + NR], start=True, stop=True)
            last.then_inc(sm["lgp"], 1)
            pe.wait_ge(sm["r_split"], 4)
            for s in range(2):
                for b in range(HALF):
                    last = nc.tensor.transpose(bank[5 + s][:, :].bitcast(BF16)[0:3 * NR, b * S:(b + 1) * S],
                                               whi[:, HALF * s + b, :, :].rearrange("p t e -> p (t e)"), identb[:, :])
                last.then_inc(sm["wTp"], 1)

            def project(k):
                s, c, u = k // NC, k % NC, k % 2
                if k >= 2:
                    pe.wait_ge(sm["e_silr"], k - 1)
                wg, wu, _ = expert(c)
                mm(bank[u][:, :], wg, nT4[:, s, :], start=True, stop=True).then_inc(sm["e_gp"], 1)
                if k >= 2:
                    pe.wait_ge(sm["e_tr"], k - 1)
                mm(bank[2 + u][:, :], wu, nT4[:, s, :], start=True, stop=True).then_inc(sm["e_up"], 1)
                if k >= 2:
                    pe.wait_ge(sm["e_hr"], k - 1)
                mm(bank[4 + u][:, :], sels[:, c * 128:(c + 1) * 128], wT[:, s * W:(s + 1) * W],
                   start=True, stop=True).then_inc(sm["e_Gp"], 1)

            def expert(c):
                return [ews[:, (3 * c + m) * 128:(3 * c + m + 1) * 128] for m in range(3)]

            pe.wait_ge(sm["wTs"], 2)
            pe.wait_ge(sm["ld_s"], 16)
            pe.wait_ge(sm["x3r"], 2)
            project(0)
            for k in range(2 * NC):
                s, c, u = k // NC, k % NC, k % 2
                if k + 1 < 2 * NC:
                    project(k + 1)
                pe.wait_ge(sm["e_hr"], k + 1)
                for b in range(HALF):
                    last = mm(bank[6 + s][:, b * D:(b + 1) * D], e_h[:, u, b * S:(b + 1) * S], expert(c)[2],
                              start=(c == 0 and b == 0), stop=(c == NC - 1), skip_group_check=True)
                last.then_inc(sm["e_yp"], 1)


def kernel(**inputs):
    import concourse.bacc as bacc
    import ml_dtypes
    from concourse.bass_utils import run_bass_kernel_spmd

    i = {k: np.asarray(v) for k, v in inputs.items()}
    f32 = np.float32

    def jdg(w):
        return w.reshape(NG, NJ, DK, -1).transpose(1, 2, 0, 3).reshape(D, -1)

    def all_rows(v):
        return np.broadcast_to(v.reshape(1, -1), (128, v.size))

    def chunks(w):
        return w.reshape(-1, 128, D).transpose(2, 0, 1)

    def down_chunks(w):
        return w.T.reshape(-1, 128, D).transpose(1, 0, 2)

    x = i["x"].transpose(1, 0, 2).reshape(S, B * D)
    ctxT = i["ctx_1024"].transpose(2, 0, 1).reshape(D, B * S)
    aw = np.concatenate([
        jdg(i["L0_xattn_w_q"]).T, jdg(i["L0_xattn_w_k"]).T, i["L0_xattn_w_v"].T, i["L0_xattn_w_o"].T,
        np.eye(128, dtype=f32), all_rows(i["L0_xattn_b_o"]), all_rows(i["L0_xattn_b_v"]), jdg(i["L0_xattn_b_q"]), jdg(i["L0_xattn_b_k"]),
        all_rows(i["g_xattn"]), all_rows(i["g_ffn"])], axis=1)
    rows = i["L1_xattn_bo"].reshape(1, D)
    fw = np.concatenate([i["L0_ffn_w_gate"].T, i["L0_ffn_w_up"].T,
                         down_chunks(i["L0_ffn_w_down"]).reshape(128, INNER)], axis=1)
    sees = (np.arange(S)[:, None] % H == np.arange(D)[None, :] // DK).astype(f32)
    lw = np.concatenate([i["L1_xattn_Wq"].T, i["L1_xattn_Wk"].T, i["L1_xattn_Wv"].T, i["L1_xattn_Wo"].T,
                         sees.T, sees, i["L1_xattn_bq"].reshape(D, 1), i["L1_xattn_bk"].reshape(D, 1),
                         i["L1_xattn_bv"].reshape(D, 1)], axis=1)
    owner = np.minimum(np.arange(NC * 128) // HID, NE)
    sel = np.tile((np.arange(NR)[:, None] == owner[None, :]), (3, 1)).astype(ml_dtypes.bfloat16)
    gate = chunks(np.concatenate([i["L1_ffn_We_gate"].reshape(NE * HID, D), i["L1_ffn_Ws_gate"]]))
    up = chunks(np.concatenate([i["L1_ffn_We_up"].reshape(NE * HID, D), i["L1_ffn_Ws_up"]]))
    down = down_chunks(np.concatenate([i["L1_ffn_We_down"].transpose(1, 0, 2).reshape(D, NE * HID),
                                       i["L1_ffn_Ws_down"]], axis=1))
    ew = np.concatenate([np.stack([gate, up, down], axis=2).reshape(128, NC * 3 * 128),
                         i["L1_ffn_Wg"].T, i["L1_ffn_Wsg"].T], axis=1)

    nc = bacc.Bacc("TRN2", target_bir_lowering=False, num_devices=1)
    arrays = dict(x=x, ctxT=ctxT, aw=aw, rows=rows, fw=fw, lw=lw, sel=sel, ew=ew)
    arrays = {f"in_{k}": np.ascontiguousarray(v) for k, v in arrays.items()}
    args = {k[3:]: nc.dram_tensor(k, v.shape, mybir.dt.from_np(v.dtype), kind="ExternalInput").ap()
            for k, v in arrays.items()}
    out = nc.dram_tensor("out_x", (S, B * D), F32, kind="ExternalOutput").ap()
    build(nc, out=out, **args)
    r = run_bass_kernel_spmd(nc, [arrays], core_ids=[0])
    return np.asarray(r.results[0]["out_x"]).reshape(S, B, D).transpose(1, 0, 2)
```

```python
from contextlib import ExitStack

import numpy as np

import concourse.bass as bass
from concourse import mybir

F32 = mybir.dt.float32
BF16 = mybir.dt.bfloat16
ALU = mybir.AluOpType
ACT = mybir.ActivationFunctionType
AX = mybir.AxisListType

B, S, D = 8, 128, 128
H, DK = 16, 8
NG, NJ = 8, 2
Q_PART = (0, 0, 1, 0, 2, 1, 1, 2)
K_PART = (0, 1, 0, 2, 0, 1, 2, 1)
NB = 4
VH = 8 * 128
DIAG = 128 + DK
INNER = 512
KEYS = 8
HALF = 4
NE, HID, SHARED = 16, 64, 256
NR = NE + 1
NC = (NE * HID + SHARED) // 128
SCALE = float(DK) ** -0.5
EPS = 1e-5
QMIN = 1e-5
MAGIC = 1.5 * 2.0 ** 23
MASKED = -1e30

A_WQ, A_WK, A_WV, A_WO, A_ID, A_BO, A_BV = (128 * k for k in range(7))
A_BQ, A_BK, A_GX, A_GF = 896, 897, 898, 900
A_COLS = 902
L_WQ, L_WK, L_WV, L_WO, L_SEES, L_BO, L_BQ = (128 * k for k in range(7))
L_BK, L_BV = 896, 897
L_COLS = 898


def build(nc, x, ctxT, aw, fw, lw, sel, ew, out):
    es = ExitStack()
    with es:
        def sb(name, shape, dt=F32):
            return es.enter_context(nc.sbuf_tensor(name, shape, dt))

        def sem(name):
            return es.enter_context(nc.semaphore(name))

        bank = [es.enter_context(nc.psum_tensor(f"bank{i}", [128, 512], F32)) for i in range(8)]

        x_all = sb("x_all", [128, B * D])
        cT = sb("cT", [128, B * S])
        a = sb("a", [128, A_COLS])
        ones_sq = sb("ones_sq", [128, 128])
        maskb = sb("maskb", [128, 128], BF16)
        identb = sb("identb", [128, 128], BF16)
        fws = sb("fws", [128, 3 * INNER])
        lws = sb("lws", [128, L_COLS])
        sels = sb("sels", [3 * NR, NC * 128], BF16)
        ews = sb("ews", [128, NC * 3 * 128 + NR])
        tg = sb("tg", [128, 4])
        stats = sb("stats", [128, B * 6])
        mv = sb("mv", [128, B * 2])
        ve = sb("ve", [128, B])
        mhalf = sb("mhalf", [128, B])
        rstd = sb("rstd", [128, B])
        ident = a[:, A_ID:A_ID + 128]

        values = sb("values", [128, B * D])
        vm = sb("vm", [128, VH + VH + 128])
        W = HALF * 128
        xn = sb("xn", [128, 2, W])
        xnT = sb("xnT", [128, 2, W])
        full = sb("full", [128, 4, W])
        rest1 = sb("rest1", [128, 4, W])
        parts = sb("parts", [128, 4, 3, W], BF16)
        qx = sb("qx", [128, NG, B * S], BF16)
        kx = sb("kx", [128, NG, NJ, B * S], BF16)
        mx = sb("mx", [128, NB, 4])
        sx = sb("sx", [128, NB, W])
        pr = sb("pr", [128, NB, W])
        pT = sb("pT", [128, 2, W])
        gbo = sb("gbo", [128, D])
        gbo3 = sb("gbo3", [128, D])
        table = sb("table", [128, 2])
        lsum = sb("lsum", [128, S])
        rl = sb("rl", [128, S])
        oT = sb("oT", [128, S])

        fabs = sb("fabs", [128, 3])
        fmean = sb("fmean", [128, 3])
        fclip = sb("fclip", [128, 3])
        fscale = sb("fscale", [128, 3])
        fdown = sb("fdown", [128, 1])
        fq32 = sb("fq32", [128, 3 * INNER])
        fq = sb("fq", [128, 3, INNER], BF16)
        kxf = kx[:, :, :, :].rearrange("p g j t -> p (g j t)").bitcast(F32)
        f_xn = kxf[:, 0:B * D]
        f_t = kxf[:, B * D:2 * B * D]
        f_xq = sb("f_xq", [128, B * D], BF16)
        f_a = sb("f_a", [128, 3, B])
        f_deq = sb("f_deq", [128, 2, B])
        f_xqT = sb("f_xqT", [128, B * S], BF16)
        f_sil = kxf[:, 2 * B * D:3 * B * D].rearrange("p (u n) -> p u n", u=2)
        f_h = kxf[:, 3 * B * D:4 * B * D].rearrange("p (u n) -> p u n", u=2)
        f_ah = sb("f_ah", [128, B, 4])
        f_ht = kxf[:, 4 * B * D:5 * B * D].rearrange("p (u n) -> p u n", u=2)
        f_hq = sb("f_hq", [128, 2, INNER], BF16)
        f_hqT = sb("f_hqT", [128, 2, INNER], BF16)

        kb, vb = xn, xnT
        kq = sb("kq", [128, 2, W])
        vo = sb("vo", [128, 2, W])
        n3, nT3 = full[:, 0:2, :], full[:, 2:4, :]
        s3 = rest1[:, 2:4, :]
        p3, pT3 = sx[:, 0:2, :], sx[:, 2:4, :]
        pn3 = pr[:, 0:2, :]
        m3 = sb("m3", [128, 2, HALF * H])
        l3 = sb("l3", [128, 2, HALF * H])
        n4 = sb("n4", [128, 2, W])
        nT4 = sb("nT4", [128, 2, W])
        lg = sb("lg", [128, B, NR])
        top8 = sb("top8", [128, B, 8])
        top2 = sb("top2", [128, B, 8])
        rest = sb("rest", [128, B, NE])
        chosen = sb("chosen", [128, B, NE])
        le = sb("le", [128, B, NR])
        ex = sb("ex", [128, B, NR])
        exc = sb("exc", [128, B, NR])
        den = sb("den", [128, B, 2])
        rden = sb("rden", [128, B, 2])
        wt = sb("wt", [128, B, NR])
        whi = sb("whi", [128, B, 3, NR], BF16)
        wr1 = sb("wr1", [128, B, NR])
        wT = sb("wT", [3 * NR, B * S], BF16)
        e_sil = full[:, 0:2, :]
        e_t = xnT
        e_h = rest1[:, 0:2, :]

        names = """ld_x ld_c0 ld_c1 ld_a ld_f ld_l ld_s ld_e stored ident_ok const_ok gates_ok v_proj v_ok
            ln_stats0 ln_stats1 ln_mv0 ln_mv1 ln_ve0 ln_ve1 ln_rstd0 ln_rstd1
            a_xn a_xT a_xTs p_proj p_full p_hi p_r1 p_mid p_lo kx_zero kx_zero1
            packed_q0 packed_q1 packed_r0 packed_r1 packed_k0 packed_k1
            gbo_ok gbo3_ok x_bo x_bo3 vm_zero vm_ok a_vm a_S a_mx a_sub a_exp a_T a_Ts a_PV a_ls a_rl a_on a_y a_res
            w_abs w_sum w_mean w_clip w_scale w_deq w_r32 w_clipd w_q
            f_xn0 f_xn1 f_xstep f_deqr f_xqr f_xqTp f_xqTs f_gp f_up f_silr f_hr f_hstep f_htr f_hqr
            f_hTp f_hTs f_yp f_res
            k3p k3s v3p v3s kqp kqs vop vos n3r t3p t3s s3p m3r s3r p3r l3r r3r pn3r pt3p pt3s y3p x3r
            n4r t4p t4s lgp lgs r_top r_two r_rest r_chosen r_le r_ex r_exc r_den r_rden r_wt r_split wTp wTs
            e_Gp e_gp e_up e_silr e_tr e_hr e_yp e_res""".split()
        sm = {n: sem(n) for n in names}
        block = es.enter_context(nc.Block())

        def diagonal(u, half):
            at = u * VH + 64 * half
            return vm[:, at:at + 8 * DIAG].rearrange("p (h e) -> p h e", e=DIAG)[:, :, 0:DK]

        def tok(t, n, w=128):
            return t[:, bass.ts(n, w)]

        def down_bank(n):
            return bank[6 if n >= HALF else 6 + n % 2]

        XSTEPS = 4
        STEPS2 = 4

        @block.sync
        def _(sp):
            sp.dma_start(x_all[:, :], x).then_inc(sm["ld_x"], 16)
            sp.dma_start(a[:, :], aw).then_inc(sm["ld_a"], 16)
            sp.dma_start(fws[:, :], fw).then_inc(sm["ld_f"], 16)
            for s in range(2):
                sp.wait_ge(sm["kx_zero1" if s else "kx_zero"], 2 - s)
                for part, done in enumerate(("p_hi", "p_mid", "p_lo")):
                    sp.wait_ge(sm[done], 2 * s + 1)
                    for r in (r for r in range(8) if K_PART[r] == part):
                        for j in range(NJ):
                            sp.dma_start(kx[16 * r + 8 * j:16 * r + 8 * j + 8, :, j, s * W:(s + 1) * W],
                                         parts[64 * j:64 * j + 64, 2 * s, part, :]).then_inc(sm[f"packed_k{s}"], 16)
                sp.wait_ge(sm["p_lo"], 2 * s + 2)
                for r in (r for r in range(8) if Q_PART[r] == 2):
                    sp.dma_start(qx[16 * r:16 * r + 16, :, s * W:(s + 1) * W],
                                 parts[:, 2 * s + 1, 2, :]).then_inc(sm[f"packed_r{s}"], 16)
            sp.dma_start(ews[:, :], ew).then_inc(sm["ld_e"], 16)
            for s in range(2):
                sp.wait_ge(sm["e_res"], s + 1)
                sp.dma_start(out[:, s * W:(s + 1) * W], x_all[:, s * W:(s + 1) * W]).then_inc(sm["stored"], 16)
            sp.wait_ge(sm["stored"], 32)

        @block.gpsimd
        def _(pool):
            nc.gpsimd.memset(identb[:, :], 0.0).then_inc(sm["ident_ok"], 1)
            nc.gpsimd.memset(maskb[:, :], 0.0).then_inc(sm["ident_ok"], 1)
            pool.wait_ge(sm["ident_ok"], 2)
            nc.gpsimd.affine_select(out=identb[:, :], in_=identb[:, :], compare_op=ALU.not_equal, fill=1.0,
                                    base=0, pattern=[[-1, 128]], channel_multiplier=1).then_inc(sm["ident_ok"], 1)
            nc.gpsimd.affine_select(out=maskb[:, :], in_=maskb[:, :], compare_op=ALU.is_ge, fill=MASKED,
                                    base=0, pattern=[[-1, 128]], channel_multiplier=1).then_inc(sm["ident_ok"], 1)
            nc.gpsimd.memset(ones_sq[:, :], 1.0).then_inc(sm["const_ok"], 1)
            nc.gpsimd.memset(mhalf[:, :], -0.5).then_inc(sm["const_ok"], 1)
            nc.gpsimd.memset(top2[:, :, :], 3e38).then_inc(sm["const_ok"], 1)
            pool.wait_ge(sm["const_ok"], 3)

            def rstd_of(r, s):
                hs = slice(s * HALF, (s + 1) * HALF)
                pool.wait_ge(sm[f"ln_mv{s}"], HALF * (r + 1))
                nc.gpsimd.tensor_scalar(ve[:, hs], mv[:, :].rearrange("p (b t) -> p b t", t=2)[:, hs, 1], EPS, None,
                                        ALU.add).then_inc(sm[f"ln_ve{s}"], 1)
                pool.wait_ge(sm[f"ln_ve{s}"], r + 1)
                nc.gpsimd.tensor_tensor(rstd[:, hs], ve[:, hs], mhalf[:, hs], ALU.pow).then_inc(sm[f"ln_rstd{s}"], 1)

            nc.gpsimd.memset(kx[:, 6:NG, :, 0:W].bitcast(F32), 0.0).then_inc(sm["kx_zero"], 1)
            nc.gpsimd.memset(vm[:, :], 0.0).then_inc(sm["vm_zero"], 1)
            rstd_of(0, 0)
            rstd_of(0, 1)
            pool.wait_ge(sm["vm_zero"], 1)
            for u in range(2):
                nc.gpsimd.memset(diagonal(u, 1 - u), 1.0).then_inc(sm["vm_ok"], 1)

            def pack_queries(s):
                for part, done in enumerate(("p_hi", "p_mid")):
                    pool.wait_ge(sm[done], 2 * s + 2)
                    for r in (r for r in range(8) if Q_PART[r] == part):
                        pool.dma_start(qx[16 * r:16 * r + 16, :, s * W:(s + 1) * W],
                                       parts[:, 2 * s + 1, part, :]).then_inc(sm[f"packed_q{s}"], 16)

            def split(m):
                pool.wait_ge(sm["p_full"], m + 1)
                nc.gpsimd.tensor_tensor(rest1[:, m, :], full[:, m, :], parts[:, m, 0, :],
                                        ALU.subtract).then_inc(sm["p_r1"], 1)
                pool.wait_ge(sm["p_r1"], m + 1)
                nc.gpsimd.tensor_copy(parts[:, m, 1, :], rest1[:, m, :]).then_inc(sm["p_mid"], 1)
                pool.wait_ge(sm["p_mid"], m + 1)
                nc.gpsimd.tensor_tensor(parts[:, m, 2, :], rest1[:, m, :], parts[:, m, 1, :],
                                        ALU.subtract).then_inc(sm["p_lo"], 1)

            pack_queries(0)
            pool.wait_ge(sm["gbo_ok"], 1)
            pool.wait_ge(sm["a_xn"], 2)
            nc.gpsimd.tensor_tensor(x_all[:, :].rearrange("p (b d) -> p b d", d=D),
                                    x_all[:, :].rearrange("p (b d) -> p b d", d=D),
                                    gbo[:, :].unsqueeze(1).to_broadcast([128, B, D]), ALU.add).then_inc(sm["x_bo"], 1)
            nc.gpsimd.memset(kx[:, :, :, W:2 * W].bitcast(F32), 0.0).then_inc(sm["kx_zero1"], 1)
            pool.wait_ge(sm["p_lo"], 2)
            split(2)
            split(3)
            pack_queries(1)
            pool.wait_ge(sm["w_scale"], 1)
            for m in range(3):
                nc.gpsimd.tensor_scalar(fq32[:, bass.ts(m, INNER)], fws[:, bass.ts(m, INNER)], fscale[:, m:m + 1],
                                        MAGIC, ALU.mult, ALU.add).then_inc(sm["w_r32"], 1)
            for m in range(3):
                pool.wait_ge(sm["w_r32"], m + 1)
                nc.gpsimd.tensor_scalar(fq32[:, bass.ts(m, INNER)], fq32[:, bass.ts(m, INNER)], MAGIC, 1.0,
                                        ALU.subtract, ALU.min).then_inc(sm["w_clipd"], 1)
            for m in range(3):
                pool.wait_ge(sm["w_clipd"], m + 1)
                nc.gpsimd.tensor_scalar(fq[:, m, :], fq32[:, bass.ts(m, INNER)], -1.0, None,
                                        ALU.max).then_inc(sm["w_q"], 1)

            rstd_of(1, 0)
            rstd_of(1, 1)
            pool.wait_ge(sm["ln_rstd1"], 2)
            for b in range(HALF, B):
                last = nc.gpsimd.tensor_scalar(tok(f_xn, b), tok(x_all, b), mv[:, 2 * b:2 * b + 1], rstd[:, b:b + 1],
                                               ALU.subtract, ALU.mult)
            last.then_inc(sm["f_xn1"], 1)
            pool.wait_ge(sm["gbo3_ok"], 1)

            def bias_into_x(s):
                pool.wait_ge(sm["n3r"], s + 1)
                xs = x_all[:, s * W:(s + 1) * W].rearrange("p (b d) -> p b d", d=D)
                nc.gpsimd.tensor_tensor(xs, xs, gbo3[:, :].unsqueeze(1).to_broadcast([128, HALF, D]),
                                        ALU.add).then_inc(sm["x_bo3"], 1)

            for s in range(2):
                rstd_of(2, s)
                bias_into_x(s)
                rstd_of(3, s)

        @block.scalar
        def _(act):
            act.dma_start(cT[:, 0:W], ctxT[:, 0:W]).then_inc(sm["ld_c0"], 16)
            act.dma_start(cT[:, W:2 * W], ctxT[:, W:2 * W]).then_inc(sm["ld_c1"], 16)
            act.dma_start(lws[:, :], lw).then_inc(sm["ld_l"], 16)
            act.dma_start(sels[:, :], sel).then_inc(sm["ld_s"], 16)
            act.wait_ge(sm["ld_a"], 16)
            nc.scalar.activation(tg[:, :], a[:, A_GX:A_GX + 4], ACT.Tanh).then_inc(sm["gates_ok"], 1)

            act.wait_ge(sm["gates_ok"], 1)
            nc.scalar.activation(gbo[:, :], a[:, A_BO:A_BO + D], ACT.Copy, scale=tg[:, 0:1]).then_inc(sm["gbo_ok"], 1)

            def project_copy(m):
                bias = a[:, A_BQ:A_BQ + 1] if m % 2 else a[:, A_BK:A_BK + 1]
                act.wait_ge(sm["p_proj"], m + 1)
                nc.scalar.activation(parts[:, m, 0, :], bank[m][:, :], ACT.Identity, bias=bias).then_inc(sm["p_hi"], 1)
                nc.scalar.activation(full[:, m, :], bank[m][:, :], ACT.Identity, bias=bias).then_inc(sm["p_full"], 1)

            def xT_copy(s):
                act.wait_ge(sm["a_xT"], s + 1)
                nc.scalar.activation(xnT[:, s, :], bank[6 + s][:, :], ACT.Copy).then_inc(sm["a_xTs"], 1)

            project_copy(0)
            xT_copy(0)
            project_copy(1)
            project_copy(2)
            xT_copy(1)
            project_copy(3)
            act.wait_ge(sm["ld_l"], 16)
            nc.scalar.activation(gbo3[:, :], lws[:, L_BO:L_BO + D], ACT.Copy,
                                 scale=tg[:, 1:2]).then_inc(sm["gbo3_ok"], 1)

            def sums_copy(n, u):
                act.wait_ge(sm["a_PV"], 4 * n + 2 * u + 2)
                nc.scalar.activation(lsum[64 * u:64 * u + 64, :], bank[6 + u][64 - 64 * u:128 - 64 * u, 0:S],
                                     ACT.Copy).then_inc(sm["a_ls"], 1)

            def exp(n, j, first=False):
                act.wait_ge(sm["a_sub"], 4 * n + j + 1)
                if not first:
                    act.wait_ge(sm["a_T"], 4 * n + j - 3)
                nc.scalar.activation(pr[:, j, :], sx[:, j, :], ACT.Exp, scale=SCALE).then_inc(sm["a_exp"], 1)

            def masked_values(n, u, first=False):
                if not first:
                    act.wait_ge(sm["a_PV"], 4 * n - 2 + 2 * u)
                nc.scalar.activation(diagonal(u, u), values[:, bass.ds(n * D + 64 * u, 64)]
                                     .rearrange("p (h e) -> p h e", e=DK), ACT.Copy).then_inc(sm["a_vm"], 1)

            def kq_copy(s):
                act.wait_ge(sm["kqp"], s + 1)
                nc.scalar.activation(kq[:, s, :], bank[s][:, :], ACT.Copy).then_inc(sm["kqs"], 1)

            def vo_copy(s):
                act.wait_ge(sm["vop"], s + 1)
                nc.scalar.activation(vo[:, s, :], bank[2 + s][:, :], ACT.Copy).then_inc(sm["vos"], 1)

            def attn(n, first, last):
                def pT_copy(j):
                    act.wait_ge(sm["a_T"], 4 * n + j + 1)
                    if not first or j >= 2:
                        act.wait_ge(sm["a_PV"], 4 * n + j - 1)
                    nc.scalar.activation(pT[:, j % 2, :], bank[4 + j % 2][:, :], ACT.Copy).then_inc(sm["a_Ts"], 1)

                pT_copy(0)
                exp(n, 3, first)
                pT_copy(1)
                masked_values(n, 1, first)
                if not last:
                    exp(n + 1, 0)
                if last:
                    kq_copy(0)
                pT_copy(2)
                if not last:
                    exp(n + 1, 1)
                else:
                    kq_copy(1)
                pT_copy(3)
                sums_copy(n, 0)
                if not last:
                    masked_values(n + 1, 0)
                    exp(n + 1, 2)
                else:
                    nc.scalar.activation(table[:, 0:1], tg[:, 0:1], ACT.Silu)
                    vo_copy(0)
                    vo_copy(1)
                sums_copy(n, 1)

            for j in range(3):
                exp(0, j, True)
            act.wait_ge(sm["v_ok"], 2)
            act.wait_ge(sm["vm_ok"], 2)
            masked_values(0, 0, True)
            attn(0, True, False)
            with act.Fori(1, B - 1) as n:
                attn(n, False, False)
            attn(B - 1, False, True)

            def xqT_copy(s):
                act.wait_ge(sm["f_xqTp"], s + 1)
                nc.scalar.activation(f_xqT[:, s * W:(s + 1) * W], bank[5 * (1 - s)][:, :].bitcast(BF16)[:, 0:W],
                                     ACT.Copy).then_inc(sm["f_xqTs"], 1)

            def silu(n):
                u = n % 2
                act.wait_ge(sm["f_gp"], n + 1)
                nc.scalar.activation(f_sil[:, u, :], bank[1 + u][:, :], ACT.Silu,
                                     scale=f_deq[:, 0, bass.ds(n, 1)]).then_inc(sm["f_silr"], 1)

            def hidden_scale(n):
                u = n % 2
                act.wait_ge(sm["f_hstep"], STEPS2 * n + 3)
                nc.scalar.activation(f_ht[:, u, :], f_h[:, u, :], ACT.Identity,
                                     scale=f_ah[:, n, 2:3]).then_inc(sm["f_htr"], 1)

            def hT_copy(n):
                u = n % 2
                act.wait_ge(sm["f_hTp"], n + 1)
                nc.scalar.activation(f_hqT[:, u, :], bank[5][:, :].bitcast(BF16)[:, 0:INNER],
                                     ACT.Copy).then_inc(sm["f_hTs"], 1)

            def xT3_copy(s):
                act.wait_ge(sm["t3p"], s + 1)
                nc.scalar.activation(nT3[:, s, :], bank[7][:, :], ACT.Copy).then_inc(sm["t3s"], 1)

            def exp3(s):
                act.wait_ge(sm["s3r"], s + 1)
                nc.scalar.activation(p3[:, s, :], s3[:, s, :], ACT.Exp, scale=SCALE).then_inc(sm["p3r"], 1)

            def pT3_copy(s):
                act.wait_ge(sm["pt3p"], s + 1)
                nc.scalar.activation(pT3[:, s, :], bank[7][:, :], ACT.Copy).then_inc(sm["pt3s"], 1)

            def xT4_copy(s):
                act.wait_ge(sm["t4p"], s + 1)
                nc.scalar.activation(nT4[:, s, :], bank[5 + 2 * s][:, :], ACT.Copy).then_inc(sm["t4s"], 1)

            def logits_copy(s):
                act.wait_ge(sm["lgp"], s + 1)
                nc.scalar.activation(lg[:, s * HALF:(s + 1) * HALF, :],
                                     bank[5 + 2 * s][:, 0:HALF * NR].rearrange("p (b e) -> p b e", e=NR),
                                     ACT.Copy).then_inc(sm["lgs"], 1)

            def router_exp(s):
                act.wait_ge(sm["r_le"], 2 * s + 2)
                nc.scalar.activation(ex[:, s * HALF:(s + 1) * HALF, :], le[:, s * HALF:(s + 1) * HALF, :],
                                     ACT.Exp).then_inc(sm["r_ex"], 1)

            def wT_copy(s):
                act.wait_ge(sm["wTp"], s + 1)
                nc.scalar.activation(wT[:, s * W:(s + 1) * W], bank[5 + 2 * s][:, :].bitcast(BF16)[0:3 * NR, 0:W],
                                     ACT.Copy).then_inc(sm["wTs"], 1)

            xqT_copy(0)
            act.wait_ge(sm["f_deqr"], 2)
            silu(0)
            silu(1)
            hidden_scale(0)
            silu(2)
            hidden_scale(1)
            silu(3)
            hT_copy(0)
            hidden_scale(2)
            hT_copy(1)

            xqT_copy(1)
            act.wait_ge(sm["f_deqr"], 4)
            silu(4)
            hidden_scale(3)
            hT_copy(2)
            silu(5)
            hT_copy(3)
            hidden_scale(4)
            silu(6)
            hidden_scale(5)
            hT_copy(4)
            xT3_copy(0)
            silu(7)
            nc.scalar.activation(table[:, 1:2], tg[:, 0:1], ACT.Exp)
            hidden_scale(6)
            hT_copy(5)
            exp3(0)
            hT_copy(6)
            pT3_copy(0)
            hidden_scale(7)
            hT_copy(7)
            xT4_copy(0)
            logits_copy(0)
            router_exp(0)
            xT3_copy(1)

            for k in range(2 * NC):
                act.wait_ge(sm["e_gp"], k + 1)
                if k >= 2:
                    act.wait_ge(sm["e_tr"], k - 1)
                nc.scalar.activation(e_sil[:, k % 2, :], bank[k % 2][:, :], ACT.Silu).then_inc(sm["e_silr"], 1)
                if k == 0:
                    wT_copy(0)
                elif k == 1:
                    exp3(1)
                elif k == 4:
                    pT3_copy(1)
                elif k == 6:
                    xT4_copy(1)
                elif k == 7:
                    logits_copy(1)
                elif k == 8:
                    router_exp(1)
                elif k == 9:
                    wT_copy(1)

        @block.vector
        def _(dve):
            V = nc.vector

            def aggregate(r, s):
                dve.wait_ge(sm[f"ln_stats{s}"], HALF * (r + 1))
                for b in range(s * HALF, (s + 1) * HALF):
                    V.bn_aggr(mv[:, 2 * b:2 * b + 2], stats[:, 6 * b:6 * b + 6]).then_inc(sm[f"ln_mv{s}"], 1)

            def wait_rstd(r, s):
                dve.wait_ge(sm[f"ln_mv{s}"], HALF * (r + 1))
                dve.wait_ge(sm[f"ln_rstd{s}"], r + 1)

            def normalize(dst, n):
                return V.tensor_scalar(dst, tok(x_all, n), mv[:, bass.ds(2 * n, 1)], rstd[:, bass.ds(n, 1)],
                                       ALU.subtract, ALU.mult)

            V.memset(kx[:, 0:6, :, 0:W].bitcast(F32), 0.0).then_inc(sm["kx_zero"], 1)
            dve.wait_ge(sm["ld_x"], 16)
            for s in range(2):
                for b in range(s * HALF, (s + 1) * HALF):
                    V.bn_stats(stats[:, 6 * b:6 * b + 6], x_all[:, b * D:(b + 1) * D]).then_inc(sm[f"ln_stats{s}"], 1)
                aggregate(0, s)

            def normalize_half(s):
                wait_rstd(0, s)
                for b in range(HALF):
                    last = normalize(xn[:, s, b * D:(b + 1) * D], HALF * s + b)
                last.then_inc(sm["a_xn"], 1)

            def split(m):
                dve.wait_ge(sm["p_full"], m + 1)
                V.tensor_tensor(rest1[:, m, :], full[:, m, :], parts[:, m, 0, :], ALU.subtract).then_inc(sm["p_r1"], 1)
                dve.wait_ge(sm["p_r1"], m + 1)
                V.tensor_copy(parts[:, m, 1, :], rest1[:, m, :]).then_inc(sm["p_mid"], 1)
                dve.wait_ge(sm["p_mid"], m + 1)
                V.tensor_tensor(parts[:, m, 2, :], rest1[:, m, :], parts[:, m, 1, :],
                                ALU.subtract).then_inc(sm["p_lo"], 1)

            def layer1_masked(s):
                for p, done, b, product, bias in (("k3p", "k3s", 6, kb, L_BK), ("v3p", "v3s", 4, vb, L_BV)):
                    dve.wait_ge(sm[p], s + 1)
                    V.scalar_tensor_tensor(product[:, s, :].rearrange("p (b t) -> p b t", b=HALF),
                                           bank[b + s][:, :].rearrange("p (b t) -> p b t", b=HALF),
                                           lws[:, bias:bias + 1],
                                           lws[:, L_SEES:L_SEES + S].unsqueeze(1).to_broadcast([128, HALF, S]),
                                           ALU.add, ALU.mult).then_inc(sm[done], 1)

            normalize_half(0)
            split(0)
            normalize_half(1)
            split(1)
            dve.wait_ge(sm["ld_f"], 16)
            V.tensor_reduce(fabs[:, :], fws[:, :].rearrange("p (m n) -> p m n", m=3), AX.X, ALU.add,
                            apply_absolute_value=True).then_inc(sm["w_abs"], 1)
            for s in range(2):
                dve.wait_ge(sm["v_proj"], s + 1)
                V.tensor_tensor(values[:, s * W:(s + 1) * W].rearrange("p (b d) -> p b d", d=D),
                                bank[4 + s][:, :].rearrange("p (b d) -> p b d", d=D),
                                a[:, A_BV:A_BV + D].unsqueeze(1).to_broadcast([128, HALF, D]),
                                ALU.add).then_inc(sm["v_ok"], 1)
            dve.wait_ge(sm["ld_l"], 16)
            layer1_masked(0)
            dve.wait_ge(sm["w_sum"], 1)
            V.tensor_scalar(fmean[:, :], bank[0][:, 0:3], 1.0 / (INNER * D), None, ALU.mult).then_inc(sm["w_mean"], 1)
            dve.wait_ge(sm["w_mean"], 1)
            V.tensor_scalar(fclip[:, :], fmean[:, :], QMIN, None, ALU.max).then_inc(sm["w_clip"], 1)
            dve.wait_ge(sm["w_clip"], 1)
            V.reciprocal(fscale[:, :], fclip[:, :]).then_inc(sm["w_scale"], 1)
            V.tensor_tensor(fdown[:, :], fclip[:, 2:3], tg[:, 2:3], ALU.mult).then_inc(sm["w_deq"], 1)
            layer1_masked(1)

            def heads_out(n):
                dve.wait_ge(sm["a_ls"], 2 * n + 2)
                V.reciprocal(rl[:, :], lsum[:, :]).then_inc(sm["a_rl"], 1)
                dve.wait_ge(sm["a_rl"], n + 1)
                for u in range(2):
                    V.tensor_tensor(oT[64 * u:64 * u + 64, :], bank[6 + u][64 * u:64 * u + 64, 0:S],
                                    rl[64 * u:64 * u + 64, :], ALU.mult).then_inc(sm["a_on"], 1)

            def residual(n):
                dve.wait_ge(sm["a_y"], n + 1)
                V.scalar_tensor_tensor(tok(x_all, n), bank[7][:, S:2 * S], tg[:, 0:1], tok(x_all, n),
                                       ALU.mult, ALU.add).then_inc(sm["a_res"], 1)

            def layer_stats(n, s):
                dve.wait_ge(sm["a_res"], n + 1)
                V.bn_stats(tok(stats, n, 6), tok(x_all, n)).then_inc(sm[f"ln_stats{s}"], 1)

            def attn(n, before, before2, half=0):
                def top(j):
                    dve.wait_ge(sm["a_S"], 4 * n + j + 1)
                    V.tensor_reduce(mx[:, j, :], bank[j][:, :].rearrange("p (h k) -> p h k", h=4), AX.X,
                                    ALU.max).then_inc(sm["a_mx"], 1)

                def sub(j):
                    dve.wait_ge(sm["a_mx"], 4 * n + j + 1)
                    if before:
                        dve.wait_ge(sm["a_exp"], 4 * n + j - 3)
                    V.tensor_tensor(sx[:, j, :].rearrange("p (h k) -> p h k", h=4),
                                    bank[j][:, :].rearrange("p (h k) -> p h k", h=4),
                                    mx[:, j, :].unsqueeze(2).to_broadcast([128, 4, S]),
                                    ALU.subtract).then_inc(sm["a_sub"], 1)

                top(0)
                sub(0)
                top(1)
                if before2:
                    residual(n - 2)
                sub(1)
                top(2)
                if before2:
                    layer_stats(n - 2, half)
                sub(2)
                top(3)
                sub(3)
                if before:
                    heads_out(n - 1)

            dve.wait_ge(sm["x_bo"], 1)
            attn(0, False, False)
            attn(1, True, False)
            with dve.Fori(2, HALF + 2) as n:
                attn(n, True, True, 0)
            with dve.Fori(HALF + 2, B) as n:
                attn(n, True, True, 1)
            aggregate(1, 0)
            residual(B - 2)
            layer_stats(B - 2, 1)

            def x_normalize(s):
                wait_rstd(1, s)
                for b in range(s * HALF, (s + 1) * HALF):
                    last = normalize(f_xn[:, b * D:(b + 1) * D], b)
                last.then_inc(sm[f"f_xn{s}"], 1)

            def x_quantize(s):
                hs = slice(s * HALF, (s + 1) * HALF)
                at = lambda k: XSTEPS * s + k - 1
                cols = lambda t: t[:, s * W:(s + 1) * W]
                seqs = lambda t: cols(t).rearrange("p (b d) -> p b d", d=D)
                dve.wait_ge(sm[f"f_xn{s}"], 1)
                V.tensor_reduce(f_a[:, 0, hs], seqs(f_xn), AX.X, ALU.max,
                                apply_absolute_value=True).then_inc(sm["f_xstep"], 1)
                dve.wait_ge(sm["f_xstep"], at(2))
                V.tensor_scalar(f_a[:, 1, hs], f_a[:, 0, hs], QMIN, 1.0 / 127.0, ALU.max, ALU.mult)\
                    .then_inc(sm["f_xstep"], 1)
                dve.wait_ge(sm["f_xstep"], at(3))
                V.reciprocal(f_a[:, 2, hs], f_a[:, 1, hs]).then_inc(sm["f_xstep"], 1)
                V.tensor_scalar(f_deq[:, 0, hs], f_a[:, 1, hs], fclip[:, 0:1], None, ALU.mult).then_inc(sm["f_deqr"], 1)
                V.tensor_scalar(f_deq[:, 1, hs], f_a[:, 1, hs], fclip[:, 1:2], None, ALU.mult).then_inc(sm["f_deqr"], 1)
                dve.wait_ge(sm["f_xstep"], at(4))
                V.tensor_tensor(seqs(f_t), seqs(f_xn), f_a[:, 2, hs].unsqueeze(2).to_broadcast([128, HALF, D]),
                                ALU.mult).then_inc(sm["f_xstep"], 1)
                dve.wait_ge(sm["f_xstep"], at(5))
                V.tensor_scalar(cols(f_xq), cols(f_t), MAGIC, MAGIC, ALU.add, ALU.subtract).then_inc(sm["f_xqr"], 1)

            x_normalize(0)
            x_quantize(0)
            heads_out(B - 1)

            def hidden_round(n):
                u = n % 2
                dve.wait_ge(sm["f_htr"], n + 1)
                V.tensor_scalar(f_hq[:, u, :], f_ht[:, u, :], MAGIC, MAGIC,
                                ALU.add, ALU.subtract).then_inc(sm["f_hqr"], 1)

            def ffn_residual(n):
                dve.wait_ge(sm["f_yp"], n + 1)
                V.scalar_tensor_tensor(tok(x_all, n), down_bank(n)[:, 0:D], f_ah[:, n, 3:4], tok(x_all, n),
                                       ALU.mult, ALU.add).then_inc(sm["f_res"], 1)

            def ffn_stats(n):
                dve.wait_ge(sm["f_res"], n + 1)
                V.bn_stats(tok(stats, n, 6), tok(x_all, n)).then_inc(sm[f"ln_stats{n // HALF}"], 1)

            def ffn(n, before, before2):
                u = n % 2
                at = lambda k: STEPS2 * n + k
                dve.wait_ge(sm["f_up"], n + 1)
                dve.wait_ge(sm["f_silr"], n + 1)
                V.scalar_tensor_tensor(f_h[:, u, :], bank[3 + u][:, :], f_deq[:, 1, bass.ds(n, 1)], f_sil[:, u, :],
                                       ALU.mult, ALU.mult).then_inc(sm["f_hr"], 1)
                dve.wait_ge(sm["f_hr"], n + 1)
                V.tensor_reduce(f_ah[:, n, 0:1], f_h[:, u, :], AX.X, ALU.max,
                                apply_absolute_value=True).then_inc(sm["f_hstep"], 1)
                dve.wait_ge(sm["f_hstep"], at(1))
                V.tensor_scalar(f_ah[:, n, 1:2], f_ah[:, n, 0:1], QMIN, 1.0 / 127.0, ALU.max, ALU.mult)\
                    .then_inc(sm["f_hstep"], 1)
                if before:
                    hidden_round(n - 1)
                dve.wait_ge(sm["f_hstep"], at(2))
                V.reciprocal(f_ah[:, n, 2:3], f_ah[:, n, 1:2]).then_inc(sm["f_hstep"], 1)
                if before2:
                    ffn_residual(n - 2)
                    ffn_stats(n - 2)
                V.tensor_scalar(f_ah[:, n, 3:4], f_ah[:, n, 1:2], fdown[:, 0:1], None,
                                ALU.mult).then_inc(sm["f_hstep"], 1)

            def layer1_normalize(r, dst, s, done):
                wait_rstd(r, s)
                for b in range(HALF):
                    last = normalize(dst[:, s, b * D:(b + 1) * D], HALF * s + b)
                last.then_inc(sm[done], 1)

            def softmax3_args(s):
                dve.wait_ge(sm["s3p"], s + 1)
                V.tensor_reduce(m3[:, s, :].rearrange("p (b h) -> p b h", h=H),
                                bank[7 * s][:, :].rearrange("p (b j h) -> p b h j", b=HALF, h=H), AX.X,
                                ALU.max).then_inc(sm["m3r"], 1)
                dve.wait_ge(sm["m3r"], s + 1)
                V.tensor_tensor(s3[:, s, :].rearrange("p (b j h) -> p b j h", b=HALF, h=H),
                                bank[7 * s][:, :].rearrange("p (b j h) -> p b j h", b=HALF, h=H),
                                m3[:, s, :].rearrange("p (b h) -> p b h", h=H).unsqueeze(2)
                                .to_broadcast([128, HALF, KEYS, H]), ALU.subtract).then_inc(sm["s3r"], 1)

            def softmax3_normalize(s):
                dve.wait_ge(sm["p3r"], s + 1)
                V.tensor_reduce(m3[:, s, :].rearrange("p (b h) -> p b h", h=H),
                                p3[:, s, :].rearrange("p (b j h) -> p b h j", b=HALF, h=H), AX.X,
                                ALU.add).then_inc(sm["l3r"], 1)
                dve.wait_ge(sm["l3r"], s + 1)
                V.reciprocal(l3[:, s, :], m3[:, s, :]).then_inc(sm["r3r"], 1)
                dve.wait_ge(sm["r3r"], s + 1)
                V.tensor_tensor(pn3[:, s, :].rearrange("p (b j h) -> p b j h", b=HALF, h=H),
                                p3[:, s, :].rearrange("p (b j h) -> p b j h", b=HALF, h=H),
                                l3[:, s, :].rearrange("p (b h) -> p b h", h=H).unsqueeze(2)
                                .to_broadcast([128, HALF, KEYS, H]), ALU.mult).then_inc(sm["pn3r"], 1)

            def residual3(s):
                dve.wait_ge(sm["y3p"], s + 1)
                dve.wait_ge(sm["x_bo3"], s + 1)
                xs = x_all[:, s * W:(s + 1) * W]
                V.scalar_tensor_tensor(xs, bank[7][:, :], tg[:, 1:2], xs, ALU.mult, ALU.add).then_inc(sm["x3r"], 1)
                dve.wait_ge(sm["x3r"], s + 1)
                for b in range(s * HALF, (s + 1) * HALF):
                    V.bn_stats(stats[:, 6 * b:6 * b + 6], x_all[:, b * D:(b + 1) * D]).then_inc(sm[f"ln_stats{s}"], 1)
                aggregate(3, s)

            def router_pick(s):
                hs = slice(s * HALF, (s + 1) * HALF)
                dve.wait_ge(sm["const_ok"], 3)
                dve.wait_ge(sm["lgs"], s + 1)
                for b in range(s * HALF, (s + 1) * HALF):
                    V.max(top8[:, b, :], lg[:, b, 0:NE]).then_inc(sm["r_top"], 1)
                V.tensor_scalar(le[:, hs, NE:NR], lg[:, hs, NE:NR], -1.0, None, ALU.mult).then_inc(sm["r_le"], 1)
                dve.wait_ge(sm["r_top"], HALF * (s + 1))
                V.tensor_tensor(le[:, hs, 0:NE], lg[:, hs, 0:NE], top8[:, hs, 0:1].to_broadcast([128, HALF, NE]),
                                ALU.subtract).then_inc(sm["r_le"], 1)
                V.tensor_copy(top2[:, hs, 0:2], top8[:, hs, 0:2]).then_inc(sm["r_two"], 1)
                dve.wait_ge(sm["r_two"], s + 1)
                for b in range(s * HALF, (s + 1) * HALF):
                    V.match_replace(rest[:, b, :], top2[:, b, :], lg[:, b, 0:NE], MASKED).then_inc(sm["r_rest"], 1)
                dve.wait_ge(sm["r_rest"], HALF * (s + 1))
                V.tensor_tensor(chosen[:, hs, :], rest[:, hs, :], lg[:, hs, 0:NE],
                                ALU.not_equal).then_inc(sm["r_chosen"], 1)

            def router_weights(s):
                hs = slice(s * HALF, (s + 1) * HALF)
                dve.wait_ge(sm["r_chosen"], s + 1)
                dve.wait_ge(sm["r_ex"], s + 1)
                V.tensor_tensor(exc[:, hs, 0:NE], ex[:, hs, 0:NE], chosen[:, hs, :], ALU.mult).then_inc(sm["r_exc"], 1)
                V.tensor_scalar(den[:, hs, 1:2], ex[:, hs, NE:NR], 1.0, None, ALU.add).then_inc(sm["r_den"], 1)
                dve.wait_ge(sm["r_exc"], s + 1)
                V.tensor_reduce(den[:, hs, 0:1], exc[:, hs, 0:NE], AX.X, ALU.add).then_inc(sm["r_den"], 1)
                dve.wait_ge(sm["r_den"], 2 * s + 2)
                V.reciprocal(rden[:, hs, :], den[:, hs, :]).then_inc(sm["r_rden"], 1)
                dve.wait_ge(sm["r_rden"], s + 1)
                V.tensor_tensor(wt[:, hs, 0:NE], exc[:, hs, 0:NE], rden[:, hs, 0:1].to_broadcast([128, HALF, NE]),
                                ALU.mult).then_inc(sm["r_wt"], 1)
                V.tensor_copy(wt[:, hs, NE:NR], rden[:, hs, 1:2]).then_inc(sm["r_wt"], 1)
                dve.wait_ge(sm["r_wt"], 2 * s + 2)
                V.tensor_copy(whi[:, hs, 0, :], wt[:, hs, :]).then_inc(sm["r_split"], 1)
                dve.wait_ge(sm["r_split"], 4 * s + 1)
                V.tensor_tensor(wr1[:, hs, :], wt[:, hs, :], whi[:, hs, 0, :], ALU.subtract).then_inc(sm["r_split"], 1)
                dve.wait_ge(sm["r_split"], 4 * s + 2)
                V.tensor_copy(whi[:, hs, 1, :], wr1[:, hs, :]).then_inc(sm["r_split"], 1)
                dve.wait_ge(sm["r_split"], 4 * s + 3)
                V.tensor_tensor(whi[:, hs, 2, :], wr1[:, hs, :], whi[:, hs, 1, :],
                                ALU.subtract).then_inc(sm["r_split"], 1)

            dve.wait_ge(sm["w_deq"], 1)
            dve.wait_ge(sm["ld_l"], 16)
            ffn(0, False, False)
            residual(B - 1)
            layer_stats(B - 1, 1)
            aggregate(1, 1)
            ffn(1, True, False)
            ffn(2, True, True)
            x_quantize(1)
            ffn(3, True, True)
            hidden_round(3)

            ffn(4, False, False)
            ffn_residual(2)
            ffn_stats(2)
            dve.wait_ge(sm["f_hstep"], STEPS2 * HALF)
            ffn_residual(3)
            ffn_stats(3)
            aggregate(2, 0)
            ffn(5, True, False)
            layer1_normalize(2, n3, 0, "n3r")
            ffn(6, True, True)
            softmax3_args(0)
            hidden_round(6)
            ffn_residual(5)
            ffn_stats(5)
            softmax3_normalize(0)
            ffn(7, False, False)
            hidden_round(7)
            dve.wait_ge(sm["f_hstep"], STEPS2 * B)
            ffn_residual(6)
            ffn_stats(6)
            residual3(0)
            ffn_residual(7)
            ffn_stats(7)
            aggregate(2, 1)
            layer1_normalize(3, n4, 0, "n4r")
            layer1_normalize(2, n3, 1, "n3r")
            router_pick(0)
            router_weights(0)

            def moe_residual(s):
                dve.wait_ge(sm["e_yp"], NC * (s + 1))
                xs = x_all[:, s * W:(s + 1) * W]
                V.scalar_tensor_tensor(xs, bank[6 + s][:, :], tg[:, 3:4], xs, ALU.mult, ALU.add)\
                    .then_inc(sm["e_res"], 1)

            for k in range(2 * NC):
                u = k % 2
                dve.wait_ge(sm["e_silr"], k + 1)
                dve.wait_ge(sm["e_up"], k + 1)
                V.tensor_tensor(e_t[:, u, :], e_sil[:, u, :], bank[2 + u][:, :], ALU.mult).then_inc(sm["e_tr"], 1)
                dve.wait_ge(sm["e_tr"], k + 1)
                dve.wait_ge(sm["e_Gp"], k + 1)
                if k >= 2:
                    dve.wait_ge(sm["e_yp"], k - 1)
                V.tensor_tensor(e_h[:, u, :], e_t[:, u, :], bank[4 + u][:, :], ALU.mult).then_inc(sm["e_hr"], 1)
                if k == 1:
                    softmax3_args(1)
                elif k == 2:
                    softmax3_normalize(1)
                elif k == 4:
                    residual3(1)
                elif k == 5:
                    layer1_normalize(3, n4, 1, "n4r")
                elif k == 7:
                    router_pick(1)
                elif k == 8:
                    router_weights(1)
                if k == NC:
                    moe_residual(0)
            moe_residual(1)

        @block.tensor
        def _(pe):
            mm = nc.tensor.matmul
            pe.wait_ge(sm["ld_a"], 16)
            pe.wait_ge(sm["const_ok"], 3)
            def q_proj(s):
                pe.wait_ge(sm["a_xn"], s + 1)
                for b in range(HALF):
                    last = nc.tensor.transpose(bank[6 + s][:, b * S:(b + 1) * S], xn[:, s, b * D:(b + 1) * D], ident)
                last.then_inc(sm["a_xT"], 1)
                pe.wait_ge(sm["a_xTs"], s + 1)
                mm(bank[2 * s + 1][:, :], a[:, A_WQ:A_WQ + D], xnT[:, s, :], start=True, stop=True)\
                    .then_inc(sm["p_proj"], 1)

            def k_proj(s):
                pe.wait_ge(sm[f"ld_c{s}"], 16)
                mm(bank[2 * s][:, :], a[:, A_WK:A_WK + D], cT[:, s * W:(s + 1) * W], start=True, stop=True)\
                    .then_inc(sm["p_proj"], 1)

            k_proj(0)
            q_proj(0)
            k_proj(1)
            q_proj(1)
            for s in range(2):
                for b in range(HALF):
                    last = mm(bank[4 + s][:, b * D:(b + 1) * D], cT[:, (HALF * s + b) * S:(HALF * s + b + 1) * S],
                              a[:, A_WV:A_WV + D], start=True, stop=True)
                last.then_inc(sm["v_proj"], 1)

            pe.wait_ge(sm["ld_l"], 16)
            for s in range(2):
                if s == 1:
                    pe.wait_ge(sm["w_abs"], 1)
                    pe.wait_ge(sm["p_full"], 1)
                    mm(bank[0][:, 0:3], ones_sq[:, :], fabs[:, :], start=True, stop=True).then_inc(sm["w_sum"], 1)
                pe.wait_ge(sm["a_xTs"], s + 1)
                mm(bank[6 + s][:, :], lws[:, L_WK:L_WK + D], cT[:, s * W:(s + 1) * W],
                   start=True, stop=True).then_inc(sm["k3p"], 1)
                pe.wait_ge(sm["v_ok"], s + 1)
                mm(bank[4 + s][:, :], lws[:, L_WV:L_WV + D], cT[:, s * W:(s + 1) * W],
                   start=True, stop=True).then_inc(sm["v3p"], 1)
            def y_proj(n):
                pe.wait_ge(sm["a_on"], 2 * n + 2)
                mm(bank[7][:, S:2 * S], oT[:, :], a[:, A_WO:A_WO + D], start=True, stop=True).then_inc(sm["a_y"], 1)

            def score(n, j, first):
                if not first:
                    pe.wait_ge(sm["a_sub"], 4 * n + j - 3)
                else:
                    pe.wait_ge(sm["p_full"], j + 1)
                mm(bank[j][:, :], identb[:, :], maskb[:, :].unsqueeze(1).to_broadcast([128, 4, S]),
                   start=True, stop=False)
                for t in range(2):
                    last = mm(bank[j][:, t * 2 * S:(t + 1) * 2 * S], qx[:, 2 * j + t, bass.ts(n, S)],
                              kx[:, 2 * j + t, :, bass.ts(n, S)], start=False, stop=(t == 1))
                last.then_inc(sm["a_S"], 1)

            def keys_times_queries(s):
                pe.wait_ge(sm["a_sub"], 4 * B - 3 + s)
                mm(bank[s][:, :], lws[:, L_WQ:L_WQ + D], kb[:, s, :], start=True, stop=True).then_inc(sm["kqp"], 1)

            def values_times_outputs(s):
                pe.wait_ge(sm["a_sub"], 4 * B - 1 + s)
                for b in range(HALF):
                    last = mm(bank[2 + s][:, b * D:(b + 1) * D], vb[:, s, b * S:(b + 1) * S],
                              lws[:, L_WO:L_WO + D], start=True, stop=True)
                last.then_inc(sm["vop"], 1)

            def attn(n, first, last_one):
                def next_score(j):
                    if not last_one:
                        score(n + 1, j, False)
                    else:
                        (keys_times_queries, values_times_outputs)[j // 2](j % 2)

                def transposes(j):
                    pe.wait_ge(sm["a_exp"], 4 * n + j + 1)
                    if not first or j >= 2:
                        pe.wait_ge(sm["a_Ts"], 4 * n + j - 1)
                    for g in range(4):
                        last = nc.tensor.transpose(bank[4 + j % 2][:, g * S:(g + 1) * S],
                                                   pr[:, j, g * S:(g + 1) * S], ident)
                    last.then_inc(sm["a_T"], 1)

                def pv(j):
                    u = j // 2
                    pe.wait_ge(sm["a_Ts"], 4 * n + j + 1)
                    if j % 2 == 0:
                        pe.wait_ge(sm["a_vm"], 2 * n + u + 1)
                        if not first:
                            if u == 0:
                                pe.wait_ge(sm["a_on"], 2 * n - 1)
                            else:
                                pe.wait_ge(sm["a_res"], n)
                    for g in range(4):
                        h = 4 * j + g
                        last = mm(bank[6 + u][:, 0:S], vm[:, h * 128:(h + 1) * 128], pT[:, j % 2, g * S:(g + 1) * S],
                                  start=(h % 8 == 0), stop=(h % 8 == 7))
                    last.then_inc(sm["a_PV"], 1)

                transposes(0)
                next_score(0)
                transposes(1)
                next_score(1)
                pv(0)
                if not first:
                    y_proj(n - 1)
                transposes(2)
                next_score(2)
                pv(1)
                transposes(3)
                next_score(3)
                pv(2)
                pv(3)

            pe.wait_ge(sm["ident_ok"], 4)
            pe.wait_ge(sm["w_mean"], 1)
            pe.wait_ge(sm["packed_k0"], 16 * 16)
            pe.wait_ge(sm["packed_q0"], 16 * 6)
            pe.wait_ge(sm["packed_r0"], 16 * 2)
            for j in range(NB):
                score(0, j, True)
            pe.wait_ge(sm["k3s"], 2)
            pe.wait_ge(sm["v3s"], 2)
            attn(0, True, False)
            with pe.Fori(1, HALF - 1) as n:
                attn(n, False, False)
            pe.wait_ge(sm["packed_k1"], 16 * 16)
            pe.wait_ge(sm["packed_q1"], 16 * 6)
            pe.wait_ge(sm["packed_r1"], 16 * 2)
            with pe.Fori(HALF - 1, B - 1) as n:
                attn(n, False, False)
            attn(B - 1, False, True)

            def xq_transposes(s):
                pe.wait_ge(sm["f_xqr"], s + 1)
                for b in range(s * HALF, (s + 1) * HALF):
                    c = b - s * HALF
                    last = nc.tensor.transpose(bank[5 * (1 - s)][:, :].bitcast(BF16)[:, c * S:(c + 1) * S],
                                               f_xq[:, b * D:(b + 1) * D], identb[:, :])
                last.then_inc(sm["f_xqTp"], 1)

            pe.wait_ge(sm["a_Ts"], 4 * B)
            xq_transposes(0)

            def gate_up(n):
                u = n % 2
                if n >= 2:
                    pe.wait_ge(sm["f_silr"], n - 1)
                    pe.wait_ge(sm["f_hr"], n - 1)
                for m, done in enumerate(("f_gp", "f_up")):
                    mm(bank[1 + 2 * m + u][:, :], f_xqT[:, bass.ts(n, S)], fq[:, m, :],
                       start=True, stop=True).then_inc(sm[done], 1)

            def h_transposes(n):
                u = n % 2
                pe.wait_ge(sm["f_hqr"], n + 1)
                if n >= 1:
                    pe.wait_ge(sm["f_hTs"], n)
                for c in range(4):
                    last = nc.tensor.transpose(bank[5][:, :].bitcast(BF16)[:, c * S:(c + 1) * S],
                                               f_hq[:, u, c * 128:(c + 1) * 128], identb[:, :])
                last.then_inc(sm["f_hTp"], 1)

            def down(n):
                u = n % 2
                pe.wait_ge(sm["f_hTs"], n + 1)
                if n >= HALF:
                    pe.wait_ge(sm["f_res"], n)
                elif n >= 2:
                    pe.wait_ge(sm["f_res"], n - 1)
                for c in range(4):
                    last = mm(down_bank(n)[:, 0:D], f_hqT[:, u, c * S:(c + 1) * S], fq[:, 2, c * D:(c + 1) * D],
                              start=(c == 0), stop=(c == 3))
                last.then_inc(sm["f_yp"], 1)

            def each(s, f):
                for b in range(HALF):
                    last = f(b, slice(b * S, (b + 1) * S))
                return last

            def x3_transposes(s):
                pe.wait_ge(sm["n3r"], s + 1)
                each(s, lambda b, c: nc.tensor.transpose(bank[7][:, c], n3[:, s, c], ident)).then_inc(sm["t3p"], 1)

            def scores3_bias(s):
                if s == 1:
                    pe.wait_ge(sm["t3s"], 2)
                mm(bank[7 * s][:, :], lws[:, L_BQ:L_BQ + 128], kb[:, s, :], start=True, stop=False)

            def scores3(s):
                pe.wait_ge(sm["t3s"], s + 1)
                each(s, lambda b, c: mm(bank[7 * s][:, c], nT3[:, s, c], kq[:, s, c],
                                        start=False, stop=(b == HALF - 1))).then_inc(sm["s3p"], 1)

            def p3_transposes(s):
                pe.wait_ge(sm["pn3r"], s + 1)
                each(s, lambda b, c: nc.tensor.transpose(bank[7][:, c], pn3[:, s, c], ident)).then_inc(sm["pt3p"], 1)

            def y3_proj(s):
                pe.wait_ge(sm["pt3s"], s + 1)
                each(s, lambda b, c: mm(bank[7][:, c], pT3[:, s, c], vo[:, s, c],
                                        start=True, stop=True)).then_inc(sm["y3p"], 1)

            def x4_transposes(s):
                pe.wait_ge(sm["n4r"], s + 1)
                pe.wait_ge(sm["x3r"] if s else sm["f_hTs"], 2 if s else B)
                each(s, lambda b, c: nc.tensor.transpose(bank[5 + 2 * s][:, c], n4[:, s, c], ident))\
                    .then_inc(sm["t4p"], 1)

            def logits(s):
                pe.wait_ge(sm["t4s"], s + 1)
                each(s, lambda b, c: mm(bank[5 + 2 * s][:, b * NR:(b + 1) * NR], nT4[:, s, c],
                                        ews[:, NC * 3 * 128:NC * 3 * 128 + NR],
                                        start=True, stop=True)).then_inc(sm["lgp"], 1)

            def w_transposes(s):
                pe.wait_ge(sm["r_split"], 4 * s + 4)
                pe.wait_ge(sm["lgs"], s + 1)
                each(s, lambda b, c: nc.tensor.transpose(
                    bank[5 + 2 * s][:, :].bitcast(BF16)[0:3 * NR, c],
                    whi[:, HALF * s + b, :, :].rearrange("p t e -> p (t e)"), identb[:, :])).then_inc(sm["wTp"], 1)

            def expert(c):
                return [ews[:, (3 * c + m) * 128:(3 * c + m + 1) * 128] for m in range(3)]

            def hidden_proj(k):
                s, c, u = k // NC, k % NC, k % 2
                if k >= 2:
                    pe.wait_ge(sm["e_silr"], k - 1)
                mm(bank[u][:, :], expert(c)[0], nT4[:, s, :], start=True, stop=True).then_inc(sm["e_gp"], 1)
                if k >= 2:
                    pe.wait_ge(sm["e_tr"], k - 1)
                mm(bank[2 + u][:, :], expert(c)[1], nT4[:, s, :], start=True, stop=True).then_inc(sm["e_up"], 1)

            def spread_weights(k):
                s, c, u = k // NC, k % NC, k % 2
                pe.wait_ge(sm["wTs"], s + 1)
                if k >= 2:
                    pe.wait_ge(sm["e_hr"], k - 1)
                mm(bank[4 + u][:, :], sels[:, c * 128:(c + 1) * 128], wT[:, s * W:(s + 1) * W],
                   start=True, stop=True).then_inc(sm["e_Gp"], 1)

            def down_proj(k):
                s, c, u = k // NC, k % NC, k % 2
                pe.wait_ge(sm["e_hr"], k + 1)
                for b in range(HALF):
                    last = mm(bank[6 + s][:, b * D:(b + 1) * D], e_h[:, u, b * S:(b + 1) * S], expert(c)[2],
                              start=(c == 0 and b == 0), stop=(c == NC - 1), skip_group_check=True)
                last.then_inc(sm["e_yp"], 1)

            pe.wait_ge(sm["w_q"], 3)
            pe.wait_ge(sm["kqs"], 2)
            pe.wait_ge(sm["vos"], 2)
            pe.wait_ge(sm["f_xqTs"], 1)
            gate_up(0)
            y_proj(B - 1)
            gate_up(1)
            gate_up(2)
            gate_up(3)
            h_transposes(0)
            down(0)
            h_transposes(1)
            down(1)
            xq_transposes(1)

            pe.wait_ge(sm["f_xqTs"], 2)
            gate_up(4)
            h_transposes(2)
            gate_up(5)
            h_transposes(3)
            down(2)
            down(3)
            scores3_bias(0)
            gate_up(6)
            h_transposes(4)
            down(4)
            x3_transposes(0)
            gate_up(7)
            scores3(0)
            h_transposes(5)
            down(5)
            h_transposes(6)
            down(6)
            p3_transposes(0)
            y3_proj(0)
            h_transposes(7)
            down(7)
            x4_transposes(0)
            pe.wait_ge(sm["ld_e"], 16)
            logits(0)
            x3_transposes(1)
            hidden_proj(0)
            w_transposes(0)
            pe.wait_ge(sm["ld_s"], 16)
            spread_weights(0)

            for k in range(2 * NC):
                if k + 1 < 2 * NC:
                    hidden_proj(k + 1)
                    spread_weights(k + 1)
                if k == 3:
                    p3_transposes(1)
                down_proj(k)
                if k == 0:
                    scores3_bias(1)
                    scores3(1)
                elif k == 3:
                    y3_proj(1)
                elif k == 5:
                    x4_transposes(1)
                elif k == 6:
                    logits(1)
                elif k == 8:
                    w_transposes(1)


def kernel(**inputs):
    import concourse.bacc as bacc
    import ml_dtypes
    from concourse.bass_utils import run_bass_kernel_spmd

    i = {k: np.asarray(v) for k, v in inputs.items()}
    f32 = np.float32

    def jdg(w):
        return w.reshape(NG, NJ, DK, -1).transpose(1, 2, 0, 3).reshape(D, -1)

    def all_rows(v):
        return np.broadcast_to(v.reshape(1, -1), (128, v.size))

    def chunks(w):
        return w.reshape(-1, 128, D).transpose(2, 0, 1)

    def down_chunks(w):
        return w.T.reshape(-1, 128, D).transpose(1, 0, 2)

    x = i["x"].transpose(1, 0, 2).reshape(S, B * D)
    ctxT = i["ctx_1024"].transpose(2, 0, 1).reshape(D, B * S)
    aw = np.concatenate([
        jdg(i["L0_xattn_w_q"]).T, jdg(i["L0_xattn_w_k"]).T, i["L0_xattn_w_v"].T, i["L0_xattn_w_o"].T,
        np.eye(128, dtype=f32), all_rows(i["L0_xattn_b_o"]), all_rows(i["L0_xattn_b_v"]),
        jdg(i["L0_xattn_b_q"]), jdg(i["L0_xattn_b_k"]),
        all_rows(i["g_xattn"]), all_rows(i["g_ffn"])], axis=1)
    fw = np.concatenate([i["L0_ffn_w_gate"].T, i["L0_ffn_w_up"].T,
                         down_chunks(i["L0_ffn_w_down"]).reshape(128, INNER)], axis=1)
    sees = (np.arange(D)[:, None] // DK == np.arange(S)[None, :] % H).astype(f32)
    lw = np.concatenate([
        i["L1_xattn_Wq"], i["L1_xattn_Wk"].T, i["L1_xattn_Wv"].T, i["L1_xattn_Wo"].T, sees,
        all_rows(i["L1_xattn_bo"]), np.broadcast_to(i["L1_xattn_bq"].reshape(D, 1), (D, 128)),
        i["L1_xattn_bk"].reshape(D, 1), i["L1_xattn_bv"].reshape(D, 1)], axis=1)
    owner = np.minimum(np.arange(NC * 128) // HID, NE)
    sel = np.tile((np.arange(NR)[:, None] == owner[None, :]), (3, 1)).astype(ml_dtypes.bfloat16)
    gate = chunks(np.concatenate([i["L1_ffn_We_gate"].reshape(NE * HID, D), i["L1_ffn_Ws_gate"]]))
    up = chunks(np.concatenate([i["L1_ffn_We_up"].reshape(NE * HID, D), i["L1_ffn_Ws_up"]]))
    down = down_chunks(np.concatenate([i["L1_ffn_We_down"].transpose(1, 0, 2).reshape(D, NE * HID),
                                       i["L1_ffn_Ws_down"]], axis=1))
    ew = np.concatenate([np.stack([gate, up, down], axis=2).reshape(128, NC * 3 * 128),
                         i["L1_ffn_Wg"].T, i["L1_ffn_Wsg"].T], axis=1)

    nc = bacc.Bacc("TRN2", target_bir_lowering=False, num_devices=1)
    arrays = dict(x=x, ctxT=ctxT, aw=aw, fw=fw, lw=lw, sel=sel, ew=ew)
    arrays = {f"in_{k}": np.ascontiguousarray(v) for k, v in arrays.items()}
    args = {k[3:]: nc.dram_tensor(k, v.shape, mybir.dt.from_np(v.dtype), kind="ExternalInput").ap()
            for k, v in arrays.items()}
    out = nc.dram_tensor("out_x", (S, B * D), F32, kind="ExternalOutput").ap()
    build(nc, out=out, **args)
    r = run_bass_kernel_spmd(nc, [arrays], core_ids=[0])
    return np.asarray(r.results[0]["out_x"]).reshape(S, B, D).transpose(1, 0, 2)
```
